# Optimizing a Trainium2 kernel written in Bass

```python
import numpy as np
import jax
import jax.numpy as jnp

def _softmax(x, axis=-1):
    return jax.nn.softmax(x, axis=axis)

def _gelu(x):
    return jax.nn.gelu(x, approximate=True)

def _silu(x):
    return jax.nn.silu(x)

def _sigmoid(x):
    return jax.nn.sigmoid(x)

def _layernorm(x, axis=-1, eps=1e-05):
    m = jnp.mean(x, axis=axis, keepdims=True)
    v = jnp.var(x, axis=axis, keepdims=True)
    return (x - m) / jnp.sqrt(v + eps)

def _scatter_add(tgt, idx, src, axis=0):
    return tgt.at[idx].add(src)

def _segment_sum(src, seg, n):
    return jax.ops.segment_sum(src, seg, n)
kernel_name = 'mk_seq_preln_d2_jaxref_r8_d59bfb'

def setup_inputs(seed: int=0):
    np.random.seed(seed)
    _w = jnp.asarray

    def _L0_attn_setup():
        import jax, jax.numpy as jnp
        import numpy as np
        HID = 256
        NK, DK = (16, 128)
        NV, DV = (32, 128)
        KC = 4
        P = NV // NK
        SV = P * DV
        QD = NK * DK
        VD = NV * DV
        QKV = QD + QD + VD
        B, T = (2, 256)
        EPS_NORM = 1e-12
        EPS_RMS = 1e-06

        def _l2norm(x):
            n = jnp.sqrt(jnp.sum(x * x, axis=-1, keepdims=True))
            return x / jnp.maximum(n, EPS_NORM)

        def _reference_tuple_inner(x, W_qkv, W_z, W_b, W_a, conv_w, dt_bias, A_log, norm_w, W_out):
            Bq, Tq, _ = x.shape
            qkv = jnp.einsum('btc,dc->btd', x, W_qkv)
            z = jnp.einsum('btc,dc->btd', x, W_z)
            beta = jax.nn.sigmoid(jnp.einsum('btc,hc->bth', x, W_b))
            dt = jax.nn.softplus(jnp.einsum('btc,hc->bth', x, W_a) + dt_bias)
            decay = jnp.exp(-dt * jnp.exp(A_log))
            xp = jnp.pad(qkv, ((0, 0), (KC - 1, 0), (0, 0)))
            qkv_c = sum((xp[:, j:j + Tq, :] * conv_w[:, j] for j in range(KC)))
            new_conv_buf = jnp.transpose(xp[:, -(KC - 1):, :], (0, 2, 1))
            q = _l2norm(qkv_c[..., :QD].reshape(Bq, Tq, NK, DK))
            k = _l2norm(qkv_c[..., QD:2 * QD].reshape(Bq, Tq, NK, DK))
            v = qkv_c[..., 2 * QD:].reshape(Bq, Tq, NK, P, DV)
            beta_r = beta.reshape(Bq, Tq, NK, P)
            decay_r = decay.reshape(Bq, Tq, NK, P)
            qT = jnp.swapaxes(q, 0, 1)
            kT = jnp.swapaxes(k, 0, 1)
            vT = jnp.swapaxes(v, 0, 1)
            bT = jnp.swapaxes(beta_r, 0, 1)
            dT = jnp.swapaxes(decay_r, 0, 1)

            def step(S, inp):
                q_t, k_t, v_t, b_t, d_t = inp
                Sk = jnp.einsum('bhi,bhipj->bhpj', k_t, S)
                dv = b_t[..., None] * (v_t - Sk)
                upd = jnp.einsum('bhi,bhpj->bhipj', k_t, dv)
                S = S * d_t[:, :, None, :, None] + upd
                o = jnp.einsum('bhi,bhipj->bhpj', q_t, S)
                return (S, o)
            S0 = jnp.zeros((Bq, NK, DK, P, DV), x.dtype)
            S_final, outs = jax.lax.scan(step, S0, (qT, kT, vT, bT, dT))
            out = jnp.swapaxes(outs, 0, 1).reshape(Bq, Tq, NV, DV)
            rms = jax.lax.rsqrt(jnp.mean(out * out, axis=-1, keepdims=True) + EPS_RMS)
            out = out * rms * norm_w
            out = out.reshape(Bq, Tq, VD) * jax.nn.silu(z)
            y = jnp.einsum('btd,cd->btc', out, W_out)
            return (y, S_final.reshape(Bq, NK, DK, SV), new_conv_buf)
        key = jax.random.key(seed)
        ks = jax.random.split(key, 8)
        lin = lambda k, o, i: jax.random.normal(k, (o, i), jnp.float32) / np.sqrt(i).astype(np.float32)
        return {'x': jax.random.normal(ks[0], (B, T, HID), jnp.float32), 'W_qkv': lin(ks[1], QKV, HID), 'W_z': lin(ks[2], VD, HID), 'W_b': lin(ks[3], NV, HID), 'W_a': lin(ks[4], NV, HID), 'conv_w': jax.random.normal(ks[5], (QKV, KC), jnp.float32) * 0.1, 'dt_bias': jnp.zeros((NV,), jnp.float32), 'A_log': jnp.zeros((NV,), jnp.float32), 'norm_w': jnp.ones((DV,), jnp.float32), 'W_out': lin(ks[6], HID, VD)}
    _L0_attn_in = _L0_attn_setup()

    def _L0_ffn_setup():
        import jax, jax.numpy as jnp
        import numpy as np
        HIDDEN = 256
        INTER = 1024
        COMPRESSION = 128.9

        def _n_ctrl(out_size, in_size):
            return max(16, int(out_size * in_size / COMPRESSION))

        def _catmull_rom_grid(n_ctrl, n_samples):
            t = np.linspace(0.0, n_ctrl - 1.0, n_samples, dtype=np.float64)
            i = np.clip(np.floor(t).astype(np.int64), 0, n_ctrl - 2)
            f = (t - i).astype(np.float32)
            idx = np.stack([np.clip(i + k, 0, n_ctrl - 1) for k in (-1, 0, 1, 2)], axis=0)
            return (jnp.asarray(idx.astype(np.int32)), jnp.asarray(f))

        def spline_reconstruct(control_points, out_size, in_size):
            n = out_size * in_size
            idx, f = _catmull_rom_grid(control_points.shape[0], n)
            p0, p1, p2, p3 = (control_points[idx[0]], control_points[idx[1]], control_points[idx[2]], control_points[idx[3]])
            f2 = f * f
            f3 = f2 * f
            w = 0.5 * (2.0 * p1 + (p2 - p0) * f + (2.0 * p0 - 5.0 * p1 + 4.0 * p2 - p3) * f2 + (3.0 * p1 - p0 - 3.0 * p2 + p3) * f3)
            return w.reshape(out_size, in_size)
        key = jax.random.key(seed)
        k0, k1, k2, k3 = jax.random.split(key, 4)
        hidden_states = jax.random.normal(k0, (4, 256, HIDDEN), dtype=jnp.float32)
        gate_cp = jax.random.normal(k1, (_n_ctrl(INTER, HIDDEN),), dtype=jnp.float32) * 0.02
        up_cp = jax.random.normal(k2, (_n_ctrl(INTER, HIDDEN),), dtype=jnp.float32) * 0.02
        down_cp = jax.random.normal(k3, (_n_ctrl(HIDDEN, INTER),), dtype=jnp.float32) * 0.02
        return {'hidden_states': hidden_states, 'gate_cp': gate_cp, 'up_cp': up_cp, 'down_cp': down_cp}
    _L0_ffn_in = _L0_ffn_setup()

    def _L1_attn_setup():
        import jax, jax.numpy as jnp
        import numpy as np
        N_KV_HEAD = 8
        GROUP_SIZE = 4
        ROPE_BASE = 10000.0

        def _rope(x):
            t, d = (x.shape[-2], x.shape[-1])
            j = jnp.arange(d // 2, dtype=jnp.float32)
            theta = jnp.asarray(ROPE_BASE, jnp.float32) ** (-2.0 * j / d)
            pos = (jnp.arange(t, dtype=jnp.float32) + 1.0)[:, None]
            ang = pos * theta[None, :]
            C = jnp.concatenate([ang, ang], axis=-1)
            x2 = jnp.concatenate([-x[..., d // 2:], x[..., :d // 2]], axis=-1)
            return x * jnp.cos(C) + x2 * jnp.sin(C)
        key = jax.random.key(seed)
        ks = jax.random.split(key, 9)
        b, t, e = (2, 256, 256)
        kv = e // GROUP_SIZE
        s_in = 1.0 / np.sqrt(e)
        return {'x': jax.random.normal(ks[0], (b, t, e), jnp.float32), 'Wq': jax.random.normal(ks[1], (e, e), jnp.float32) * s_in, 'bq': jax.random.normal(ks[2], (e,), jnp.float32) * 0.01, 'Wk': jax.random.normal(ks[3], (kv, e), jnp.float32) * s_in, 'bk': jax.random.normal(ks[4], (kv,), jnp.float32) * 0.01, 'Wv': jax.random.normal(ks[5], (kv, e), jnp.float32) * s_in, 'bv': jax.random.normal(ks[6], (kv,), jnp.float32) * 0.01, 'Wo': jax.random.normal(ks[7], (e, e), jnp.float32) * s_in, 'bo': jax.random.normal(ks[8], (e,), jnp.float32) * 0.01}
    _L1_attn_in = _L1_attn_setup()

    def _L1_ffn_setup():
        import jax, jax.numpy as jnp
        import numpy as np
        DIM = 256
        HID = 704
        ZERO_POINT = 128.0

        def _qlinear(x, wq, scale):
            W = (wq.astype(jnp.float32) - ZERO_POINT) * scale[:, None]
            return jnp.einsum('bsd,hd->bsh', x, W)
        key = jax.random.key(seed)
        ks = jax.random.split(key, 7)
        B, S = (4, 256)
        sg = jax.random.uniform(ks[1], (HID,)) * (0.02 / np.sqrt(DIM)) + 0.0001
        su = jax.random.uniform(ks[3], (HID,)) * (0.02 / np.sqrt(DIM)) + 0.0001
        sd = jax.random.uniform(ks[5], (DIM,)) * (0.02 / np.sqrt(HID)) + 0.0001
        return {'x': jax.random.normal(ks[0], (B, S, DIM), dtype=jnp.float32), 'wq_gate': jax.random.randint(ks[2], (HID, DIM), 0, 32, dtype=jnp.int32), 's_gate': sg, 'wq_up': jax.random.randint(ks[4], (HID, DIM), 0, 32, dtype=jnp.int32), 's_up': su, 'wq_down': jax.random.randint(ks[6], (DIM, HID), 0, 32, dtype=jnp.int32), 's_down': sd}
    _L1_ffn_in = _L1_ffn_setup()
    _d = {'L0_attn_x': _L0_attn_in['x'], 'L0_attn_W_qkv': _L0_attn_in['W_qkv'], 'L0_attn_W_z': _L0_attn_in['W_z'], 'L0_attn_W_b': _L0_attn_in['W_b'], 'L0_attn_W_a': _L0_attn_in['W_a'], 'L0_attn_conv_w': _L0_attn_in['conv_w'], 'L0_attn_dt_bias': _L0_attn_in['dt_bias'], 'L0_attn_A_log': _L0_attn_in['A_log'], 'L0_attn_norm_w': _L0_attn_in['norm_w'], 'L0_attn_W_out': _L0_attn_in['W_out'], 'L0_ffn_gate_cp': _L0_ffn_in['gate_cp'], 'L0_ffn_up_cp': _L0_ffn_in['up_cp'], 'L0_ffn_down_cp': _L0_ffn_in['down_cp'], 'L1_attn_Wq': _L1_attn_in['Wq'], 'L1_attn_bq': _L1_attn_in['bq'], 'L1_attn_Wk': _L1_attn_in['Wk'], 'L1_attn_bk': _L1_attn_in['bk'], 'L1_attn_Wv': _L1_attn_in['Wv'], 'L1_attn_bv': _L1_attn_in['bv'], 'L1_attn_Wo': _L1_attn_in['Wo'], 'L1_attn_bo': _L1_attn_in['bo'], 'L1_ffn_wq_gate': _L1_ffn_in['wq_gate'], 'L1_ffn_s_gate': _L1_ffn_in['s_gate'], 'L1_ffn_wq_up': _L1_ffn_in['wq_up'], 'L1_ffn_s_up': _L1_ffn_in['s_up'], 'L1_ffn_wq_down': _L1_ffn_in['wq_down'], 'L1_ffn_s_down': _L1_ffn_in['s_down']}
    _x0 = _d['L0_attn_x']
    _d['L0_attn_x'] = jax.random.normal(jax.random.fold_in(jax.random.key(seed), 1), (4, 512, 256), dtype=_x0.dtype)
    del _x0
    return _d

def reference(L0_attn_x, L0_attn_W_qkv, L0_attn_W_z, L0_attn_W_b, L0_attn_W_a, L0_attn_conv_w, L0_attn_dt_bias, L0_attn_A_log, L0_attn_norm_w, L0_attn_W_out, L0_ffn_gate_cp, L0_ffn_up_cp, L0_ffn_down_cp, L1_attn_Wq, L1_attn_bq, L1_attn_Wk, L1_attn_bk, L1_attn_Wv, L1_attn_bv, L1_attn_Wo, L1_attn_bo, L1_ffn_wq_gate, L1_ffn_s_gate, L1_ffn_wq_up, L1_ffn_s_up, L1_ffn_wq_down, L1_ffn_s_down):

    def _L0_attn_ref(x, W_qkv, W_z, W_b, W_a, conv_w, dt_bias, A_log, norm_w, W_out):
        import jax, jax.numpy as jnp
        import numpy as np
        HID = 256
        NK, DK = (16, 128)
        NV, DV = (32, 128)
        KC = 4
        P = NV // NK
        SV = P * DV
        QD = NK * DK
        VD = NV * DV
        QKV = QD + QD + VD
        B, T = (2, 256)
        EPS_NORM = 1e-12
        EPS_RMS = 1e-06

        def _l2norm(x):
            n = jnp.sqrt(jnp.sum(x * x, axis=-1, keepdims=True))
            return x / jnp.maximum(n, EPS_NORM)

        def _reference_tuple_inner(x, W_qkv, W_z, W_b, W_a, conv_w, dt_bias, A_log, norm_w, W_out):
            Bq, Tq, _ = x.shape
            qkv = jnp.einsum('btc,dc->btd', x, W_qkv)
            z = jnp.einsum('btc,dc->btd', x, W_z)
            beta = jax.nn.sigmoid(jnp.einsum('btc,hc->bth', x, W_b))
            dt = jax.nn.softplus(jnp.einsum('btc,hc->bth', x, W_a) + dt_bias)
            decay = jnp.exp(-dt * jnp.exp(A_log))
            xp = jnp.pad(qkv, ((0, 0), (KC - 1, 0), (0, 0)))
            qkv_c = sum((xp[:, j:j + Tq, :] * conv_w[:, j] for j in range(KC)))
            new_conv_buf = jnp.transpose(xp[:, -(KC - 1):, :], (0, 2, 1))
            q = _l2norm(qkv_c[..., :QD].reshape(Bq, Tq, NK, DK))
            k = _l2norm(qkv_c[..., QD:2 * QD].reshape(Bq, Tq, NK, DK))
            v = qkv_c[..., 2 * QD:].reshape(Bq, Tq, NK, P, DV)
            beta_r = beta.reshape(Bq, Tq, NK, P)
            decay_r = decay.reshape(Bq, Tq, NK, P)
            qT = jnp.swapaxes(q, 0, 1)
            kT = jnp.swapaxes(k, 0, 1)
            vT = jnp.swapaxes(v, 0, 1)
            bT = jnp.swapaxes(beta_r, 0, 1)
            dT = jnp.swapaxes(decay_r, 0, 1)

            def step(S, inp):
                q_t, k_t, v_t, b_t, d_t = inp
                Sk = jnp.einsum('bhi,bhipj->bhpj', k_t, S)
                dv = b_t[..., None] * (v_t - Sk)
                upd = jnp.einsum('bhi,bhpj->bhipj', k_t, dv)
                S = S * d_t[:, :, None, :, None] + upd
                o = jnp.einsum('bhi,bhipj->bhpj', q_t, S)
                return (S, o)
            S0 = jnp.zeros((Bq, NK, DK, P, DV), x.dtype)
            S_final, outs = jax.lax.scan(step, S0, (qT, kT, vT, bT, dT))
            out = jnp.swapaxes(outs, 0, 1).reshape(Bq, Tq, NV, DV)
            rms = jax.lax.rsqrt(jnp.mean(out * out, axis=-1, keepdims=True) + EPS_RMS)
            out = out * rms * norm_w
            out = out.reshape(Bq, Tq, VD) * jax.nn.silu(z)
            y = jnp.einsum('btd,cd->btc', out, W_out)
            return (y, S_final.reshape(Bq, NK, DK, SV), new_conv_buf)
        return _reference_tuple_inner(x, W_qkv, W_z, W_b, W_a, conv_w, dt_bias, A_log, norm_w, W_out)[0]

    def _L0_ffn_ref(hidden_states, gate_cp, up_cp, down_cp):
        import jax, jax.numpy as jnp
        import numpy as np
        HIDDEN = 256
        INTER = 1024
        COMPRESSION = 128.9

        def _n_ctrl(out_size, in_size):
            return max(16, int(out_size * in_size / COMPRESSION))

        def _catmull_rom_grid(n_ctrl, n_samples):
            t = np.linspace(0.0, n_ctrl - 1.0, n_samples, dtype=np.float64)
            i = np.clip(np.floor(t).astype(np.int64), 0, n_ctrl - 2)
            f = (t - i).astype(np.float32)
            idx = np.stack([np.clip(i + k, 0, n_ctrl - 1) for k in (-1, 0, 1, 2)], axis=0)
            return (jnp.asarray(idx.astype(np.int32)), jnp.asarray(f))

        def spline_reconstruct(control_points, out_size, in_size):
            n = out_size * in_size
            idx, f = _catmull_rom_grid(control_points.shape[0], n)
            p0, p1, p2, p3 = (control_points[idx[0]], control_points[idx[1]], control_points[idx[2]], control_points[idx[3]])
            f2 = f * f
            f3 = f2 * f
            w = 0.5 * (2.0 * p1 + (p2 - p0) * f + (2.0 * p0 - 5.0 * p1 + 4.0 * p2 - p3) * f2 + (3.0 * p1 - p0 - 3.0 * p2 + p3) * f3)
            return w.reshape(out_size, in_size)
        gate_w = spline_reconstruct(gate_cp, INTER, HIDDEN)
        up_w = spline_reconstruct(up_cp, INTER, HIDDEN)
        down_w = spline_reconstruct(down_cp, HIDDEN, INTER)
        gate = jnp.einsum('bsh,ih->bsi', hidden_states, gate_w)
        up = jnp.einsum('bsh,ih->bsi', hidden_states, up_w)
        inter = jax.nn.silu(gate) * up
        return jnp.einsum('bsi,hi->bsh', inter, down_w)

    def _L1_attn_ref(x, Wq, bq, Wk, bk, Wv, bv, Wo, bo):
        import jax, jax.numpy as jnp
        import numpy as np
        N_KV_HEAD = 8
        GROUP_SIZE = 4
        ROPE_BASE = 10000.0

        def _rope(x):
            t, d = (x.shape[-2], x.shape[-1])
            j = jnp.arange(d // 2, dtype=jnp.float32)
            theta = jnp.asarray(ROPE_BASE, jnp.float32) ** (-2.0 * j / d)
            pos = (jnp.arange(t, dtype=jnp.float32) + 1.0)[:, None]
            ang = pos * theta[None, :]
            C = jnp.concatenate([ang, ang], axis=-1)
            x2 = jnp.concatenate([-x[..., d // 2:], x[..., :d // 2]], axis=-1)
            return x * jnp.cos(C) + x2 * jnp.sin(C)
        b, t, e = x.shape
        h, g = (N_KV_HEAD, GROUP_SIZE)
        d = e // (h * g)
        q = x @ Wq.T + bq
        k = x @ Wk.T + bk
        v = x @ Wv.T + bv
        q = q.reshape(b, t, h, g, d).transpose(0, 3, 2, 1, 4)
        k = k.reshape(b, t, h, d).transpose(0, 2, 1, 3)
        v = v.reshape(b, t, h, d).transpose(0, 2, 1, 3)
        q = _rope(q)
        k = _rope(k)
        scale = jnp.asarray(np.sqrt(d), x.dtype)
        att = jnp.einsum('bghqd,bhkd->bghqk', q, k) / scale
        causal = jnp.tril(jnp.ones((t, t), bool))
        att = jnp.where(causal, att, -jnp.inf)
        att = jax.nn.softmax(att, axis=-1)
        y = jnp.einsum('bghqk,bhkd->bghqd', att, v)
        y = y.transpose(0, 3, 2, 1, 4).reshape(b, t, e)
        return y @ Wo.T + bo

    def _L1_ffn_ref(x, wq_gate, s_gate, wq_up, s_up, wq_down, s_down):
        import jax, jax.numpy as jnp
        import numpy as np
        DIM = 256
        HID = 704
        ZERO_POINT = 128.0

        def _qlinear(x, wq, scale):
            W = (wq.astype(jnp.float32) - ZERO_POINT) * scale[:, None]
            return jnp.einsum('bsd,hd->bsh', x, W)
        gate = _qlinear(x, wq_gate, s_gate)
        gate = jax.nn.silu(gate)
        up = _qlinear(x, wq_up, s_up)
        return _qlinear(gate * up, wq_down, s_down)
    x = L0_attn_x
    x = x + _L0_attn_ref(_layernorm(x, axis=-1), L0_attn_W_qkv, L0_attn_W_z, L0_attn_W_b, L0_attn_W_a, L0_attn_conv_w, L0_attn_dt_bias, L0_attn_A_log, L0_attn_norm_w, L0_attn_W_out)
    x = x + _L0_ffn_ref(_layernorm(x, axis=-1), L0_ffn_gate_cp, L0_ffn_up_cp, L0_ffn_down_cp)
    x = x + _L1_attn_ref(_layernorm(x, axis=-1), L1_attn_Wq, L1_attn_bq, L1_attn_Wk, L1_attn_bk, L1_attn_Wv, L1_attn_bv, L1_attn_Wo, L1_attn_bo)
    x = x + _L1_ffn_ref(_layernorm(x, axis=-1), L1_ffn_wq_gate, L1_ffn_s_gate, L1_ffn_wq_up, L1_ffn_s_up, L1_ffn_wq_down, L1_ffn_s_down)
    return x

_drawn_inputs = setup_inputs


def setup_inputs(seed=0):
    import zlib

    import numpy as np

    out = dict(_drawn_inputs(seed))
    spreads = {'L0_attn_dt_bias': (0.0, 0.535),
     'L0_attn_A_log': (0.0, 0.304),
     'L0_attn_norm_w': (1.0, 0.2)}
    factors = {'L0_ffn_gate_cp': 2.835,
     'L0_ffn_up_cp': 3.155,
     'L0_ffn_down_cp': 3.406,
     'L1_attn_bq': 38.231,
     'L1_attn_bk': 40.239,
     'L1_attn_bv': 6.161,
     'L1_attn_bo': 6.955,
     'L1_ffn_s_gate': 8.0,
     'L1_ffn_s_up': 8.0,
     'L1_ffn_s_down': 8.0}
    for name, (base, spread) in spreads.items():
        noise = np.random.default_rng([zlib.crc32(name.encode()), seed]).standard_normal(out[name].shape)
        drawn = base * np.exp(spread * noise) if base else spread * noise
        out[name] = jnp.asarray(drawn.astype(out[name].dtype))
    for name, factor in factors.items():
        out[name] = (out[name] * factor).astype(out[name].dtype)
    return out
```

```python
from contextlib import ExitStack

import numpy as np

import concourse.bass as bass
from concourse import mybir

FP32 = mybir.dt.float32
BF16 = mybir.dt.bfloat16
INT32 = mybir.dt.int32
ALU = mybir.AluOpType
ACT = mybir.ActivationFunctionType
AX = mybir.AxisListType

P = 128
B, T, C = 4, 512, 256
TILES = B * T // P
CH = T // P
CK = C // P
NK, NV, D = 16, 32, 128
HH = NV // NK
TAPS = 4
U = CH * HH
GU = U // 2
LEVELS = [2, 4, 8, 16, 32, 64]
HALF = P // 2
ITERS = NK * B
KT, QT, V0 = 0, 1, 2
NCV, NPJ = 4, 6
LN_EPS, RMS_EPS, NORM_EPS = 1e-5, 1e-6, 1e-12

G_LOG, G_NPREV, G_INCL, G_REST, G_BETA, G_TOTAL = range(6)
NG = 6
UPTO, BEFORE, AFTER, ALL = range(4)


def layer_norm(nc, ctx, sem, name, x, xnT, ident, banks):
    def sb(n, shape):
        return ctx.enter_context(nc.sbuf_tensor(f"{name}_{n}", shape, FP32))
    stats = sb("stats", [P, 2, CH, 6])
    mv = sb("mv", [P, 2, CH, 2])
    ve = sb("ve", [P, 2, CH])
    rstd = sb("rstd", [P, 2, CH])
    xn = sb("xn", [P, 2, CH, C])
    half = sb("neghalf", [P, CH])
    stats_done, var_ready, rstd_ready = sem(name + "_stats"), sem(name + "_var"), sem(name + "_rstd")
    xn_ready, turned, stored, const = sem(name + "_xn"), sem(name + "_turned"), sem(name + "_stored"), sem(name + "_const")

    def vector(dve, before=lambda b: None):
        def statistics(b):
            before(b)
            for j in range(CH):
                last = nc.vector.bn_stats(stats[:, b % 2, j, :], x[:, (CH * b + j) * C:(CH * b + j + 1) * C])
            last.then_inc(stats_done, 1)
            dve.wait_ge(stats_done, 2 * b + 1)
            for j in range(CH):
                last = nc.vector.bn_aggr(mv[:, b % 2, j, :], stats[:, b % 2, j, :])
            last.then_inc(stats_done, 1)
            dve.wait_ge(stats_done, 2 * b + 2)
            nc.vector.tensor_scalar(ve[:, b % 2, :], mv[:, b % 2, :, 1], LN_EPS, None, ALU.add).then_inc(var_ready, 1)

        def normalise(b):
            dve.wait_ge(rstd_ready, b + 1)
            if b >= 2:
                dve.wait_ge(turned, b - 1)
            for j in range(CH):
                last = nc.vector.tensor_scalar(xn[:, b % 2, j, :], x[:, (CH * b + j) * C:(CH * b + j + 1) * C], mv[:, b % 2, j, 0:1],
                                               rstd[:, b % 2, j:j + 1], ALU.subtract, ALU.mult)
            last.then_inc(xn_ready, 1)
        statistics(0)
        for b in range(B):
            if b + 1 < B:
                statistics(b + 1)
            normalise(b)

    def gpsimd(pool):
        nc.gpsimd.memset(half[:], -0.5).then_inc(const, 1)
        pool.wait_ge(const, 1)
        for b in range(B):
            pool.wait_ge(var_ready, b + 1)
            if b >= 2:
                pool.wait_ge(xn_ready, b - 1)
            nc.gpsimd.tensor_tensor(rstd[:, b % 2, :], ve[:, b % 2, :], half[:], ALU.pow).then_inc(rstd_ready, 1)

    def tensor(pe):
        for b in range(B):
            pe.wait_ge(xn_ready, b + 1)
            if b >= 2:
                pe.wait_ge(stored, CK * (b - 1))
            for h in range(CK):
                for j in range(CH):
                    last = nc.tensor.transpose(banks[2 * (b % 2) + h][:, j * P:(j + 1) * P],
                                               xn[:, b % 2, j, h * P:(h + 1) * P], ident[:])
            last.then_inc(turned, 1)

    def scalar(act):
        for b in range(B):
            act.wait_ge(turned, b + 1)
            for h in range(CK):
                nc.scalar.activation(xnT[:, h, b * T:(b + 1) * T], banks[2 * (b % 2) + h][:], ACT.Copy).then_inc(stored, 1)

    return vector, gpsimd, tensor, scalar, stored


def first_norm_and_gates(nc, sem, banks, keep, ins):
    x, xnT, gates, wout, ident, convw = (keep[k] for k in ("x", "xnT", "gates", "wout", "ident", "convw"))
    tri, ones1 = keep["tri"], keep["ones1"]
    with ExitStack() as ctx:
        def sb(n, shape, dt=FP32):
            return ctx.enter_context(nc.sbuf_tensor("p1_" + n, shape, dt))
        N = ITERS * U
        wab = sb("wab", [P, CK, 2 * NV])
        dtb = sb("dtb", [P, NV])
        expa = sb("expa", [P, NV])
        normw = sb("normw", [P, 1])
        nb, na, ga, lg, mx = (sb(n, [P, N]) for n in ("nb", "na", "ga", "lg", "mx"))
        loaded, x_loaded = sem("p1_loaded"), sem("p1_x_loaded")
        act_step, dve_step, pe_step = sem("p1_act"), sem("p1_dve"), sem("p1_pe")
        v, g, t, s, stored = layer_norm(nc, ctx, sem, "ln1", x, xnT, ident, banks[0:4])
        loads = [(ident[:], ins["ident"]), (wab[:], ins["w_ab"]), (convw[:, 0:NK * NCV * TAPS], ins["conv_w"]), (tri[:], ins["tri"]),
                 (keep["lmask"][:], ins["lmask"]),
                 (keep["first_mask"][:], ins["first_mask"]), (normw[:], ins["norm_w"]), (dtb[:], ins["dt_bias"].partition_broadcast(P)),
                 (expa[:], ins["A_log"].partition_broadcast(P)), (wout[:, HH * C:], ins["w_out"])]
        ALL_LOADED = 16 * len(loads)

        def by_head(a):
            return a.rearrange("p (k t e) -> p k t e", k=NK, e=HH)

        def quantity(q):
            return gates[:, 0:ITERS * NG * U].rearrange("p (i q u) -> p i q u", q=NG, u=U)[:, :, q, :]

        def flat(a):
            return a.rearrange("p (i u) -> p i u", u=U)
        block = ctx.enter_context(nc.Block())

        @block.sync
        def _(sp):
            for b in range(B):
                sp.dma_start(x[:, CH * b * C:CH * (b + 1) * C].rearrange("p (j c) -> p j c", c=C),
                             ins["x"][b * T:(b + 1) * T, :].rearrange("(j p) c -> p j c", p=P)).then_inc(x_loaded, 16)

        @block.scalar
        def _(act):
            for dst, src in loads:
                act.dma_start(dst, src).then_inc(loaded, 16)
            s(act)
            act.wait_ge(dve_step, 1)
            nc.scalar.activation(nb[:], nb[:], ACT.Exp, scale=-1.0).then_inc(act_step, 1)
            act.wait_ge(loaded, ALL_LOADED)
            nc.scalar.activation(expa[:], expa[:], ACT.Exp).then_inc(act_step, 1)
            act.wait_ge(dve_step, 2)
            nc.scalar.activation(ga[:], na[:], ACT.Abs).then_inc(act_step, 1)
            act.wait_ge(act_step, 3)
            nc.scalar.activation(ga[:], ga[:], ACT.Exp, scale=-1.0).then_inc(act_step, 1)
            act.wait_ge(act_step, 4)
            nc.scalar.activation(ga[:], ga[:], ACT.Ln, bias=1.0).then_inc(act_step, 1)
            for n, q in enumerate((G_NPREV, G_INCL, G_REST, G_TOTAL)):
                act.wait_ge(pe_step, 2 + n)
                nc.scalar.activation(quantity(q), flat(banks[4 + n][:]), ACT.Exp).then_inc(act_step, 1)

        @block.gpsimd
        def _(pool):
            nc.gpsimd.memset(ones1[:], 1.0)
            nc.gpsimd.memset(convw[:, NK * NCV * TAPS:], 0.0)
            nc.gpsimd.memset(gates[:, ITERS * NG * U:], 0.0)
            nc.gpsimd.memset(wout[:, 0:HH * C], 0.0)
            g(pool)

        @block.tensor
        def _(pe):
            pe.wait_ge(loaded, ALL_LOADED)
            t(pe)
            pe.wait_ge(stored, CK * B)
            for tt in range(TILES):
                for h in range(CK):
                    last = nc.tensor.matmul(banks[4 + tt // 8][:, (tt % 8) * 2 * NV:(tt % 8 + 1) * 2 * NV],
                                            xnT[:, h, tt * P:(tt + 1) * P], wab[:, h, :], start=(h == 0), stop=(h == CK - 1))
            last.then_inc(pe_step, 1)
            pe.wait_ge(dve_step, 5)
            for n, w in enumerate((BEFORE, UPTO, AFTER, ALL)):
                nc.tensor.matmul(banks[4 + n][:], tri[:, w, :], lg[:], start=True, stop=True).then_inc(pe_step, 1)

        @block.vector
        def _(dve):
            v(dve, lambda b: dve.wait_ge(x_loaded, 16 * B))
            dve.wait_ge(loaded, ALL_LOADED)
            dve.wait_ge(pe_step, 1)
            for n, dst in enumerate((nb, na)):
                for k in range(2):
                    last = nc.vector.tensor_copy(by_head(dst[:])[:, :, 8 * k:8 * k + 8, :],
                                                 banks[4 + k][:].rearrange("p (t w k e) -> p w k t e", w=2, k=NK, e=HH)[:, n])
            last.then_inc(dve_step, 1)
            dve.wait_ge(dve_step, 1)
            nc.vector.tensor_tensor(by_head(na[:]), by_head(na[:]),
                                    dtb[:].rearrange("p (k e) -> p k e", e=HH).unsqueeze(2).broadcast_to((P, NK, TILES, HH)),
                                    ALU.add).then_inc(dve_step, 1)
            dve.wait_ge(dve_step, 2)
            nc.vector.tensor_scalar(mx[:], na[:], 0.0, None, ALU.max).then_inc(dve_step, 1)
            dve.wait_ge(act_step, 5)
            dve.wait_ge(dve_step, 3)
            nc.vector.scalar_tensor_tensor(mx[:], mx[:], -1.0, ga[:], ALU.mult, ALU.subtract).then_inc(dve_step, 1)
            dve.wait_ge(dve_step, 4)
            nc.vector.tensor_tensor(by_head(lg[:]), by_head(mx[:]),
                                    expa[:].rearrange("p (k e) -> p k e", e=HH).unsqueeze(2).broadcast_to((P, NK, TILES, HH)),
                                    ALU.mult).then_inc(dve_step, 1)
            dve.wait_ge(dve_step, 5)
            nc.vector.tensor_copy(quantity(G_LOG), flat(lg[:]))
            nc.vector.tensor_copy(keep["eye_b"][:], ident[:])
            nc.vector.tensor_scalar(keep["negmask"][:].rearrange("p (u t) -> p u t", u=GU), tri[:, AFTER, :].unsqueeze(1).broadcast_to((P, GU, P)),
                                    -30000.0, None, ALU.mult)
            nc.vector.tensor_scalar(keep["cmask"][:], tri[:, BEFORE, :], -1e30, None, ALU.mult)
            nc.vector.tensor_scalar(nb[:], nb[:], 1.0, None, ALU.add).then_inc(dve_step, 1)
            dve.wait_ge(dve_step, 6)
            nc.vector.reciprocal(quantity(G_BETA), flat(nb[:]))
            nc.vector.tensor_scalar(wout[:, HH * C:], wout[:, HH * C:], normw[:, 0:1], 0.5, ALU.mult, ALU.mult)
            dve.wait_ge(act_step, 9)
            nc.vector.tensor_scalar(quantity(G_NPREV), quantity(G_NPREV), -1.0, None, ALU.mult)


def delta_rule(nc, sem, banks, keep, ins):
    x, xnT, gates, wout, ident, convw = (keep[k] for k in ("x", "xnT", "gates", "wout", "ident", "convw"))
    tri, negmask, eye_b, first_mask, lmask, ones1 = (keep[k] for k in ("tri", "negmask", "eye_b", "first_mask", "lmask", "ones1"))
    with ExitStack() as ctx:
        def sb(n, shape, dt=FP32):
            return ctx.enter_context(nc.sbuf_tensor("gd_" + n, shape, dt))
        w = sb("w", [P, CK, NPJ * D])
        raw = sb("raw", [P, NCV, TAPS - 1 + T])
        cv = [sb(f"cv{i}", [P, NCV, T]) for i in range(2)]
        zs = [sb(f"zs{i}", [P, HH, T]) for i in range(2)]
        zt = sb("zt", [P, HH, T])
        sq = sb("sq", [P, 2, T])
        gt = [sb(f"gt{i}", [P, NG, U]) for i in range(2)]
        gm = sb("gm", [P, U, P])
        n2 = [sb(f"n2{i}", [P, CH, 2]) for i in range(2)]
        nk = sb("nk", [P, CH])
        rk2 = sb("rk2", [P, CH])
        cs = sb("cs", [P, U])
        cr = sb("cr", [P, U])
        halves = sb("halves", [P, 2, U])
        ktok = sb("ktok", [P, CH, D])
        vn = sb("vn", [P, U, D])
        E = sb("E", [P, U, 1 + P])
        Lt = sb("Lt", [P, U, P])
        attT = sb("attT", [P, U, P])
        X = sb("X", [P, U, P])
        XT = sb("XT", [P, U, P])
        T1 = sb("T1", [P, 2, GU, HALF])
        S = sb("S", [P, HH, D])
        R = sb("R", [P, HH, D])
        uh = sb("uh", [P, HH, D])
        us = sb("us", [P, HH, D])
        qss = sb("qss", [P, HH, D])
        O = sb("O", [P, U, D])
        junk = sb("junk", [P, U, D])
        ssq = sb("ssq", [P, U])
        eq = sb("eq", [P, CH])
        ms = sb("ms", [P, U])
        rms = sb("rms", [P, U])
        gated = sb("gated", [P, HH, T])
        PJ = [banks[0], banks[1]]
        INV = [banks[2], banks[3]]
        TRX = [banks[4], banks[5]]
        KS, QS, UB, OB = banks[2:6]
        LOW = [banks[6], banks[7]]

        s_ = lambda n: sem("gd_" + n)
        inits = s_("inits")
        w_loaded = s_("w_loaded")
        projected, copied = s_("projected"), s_("copied")
        tanh_done, z_ready = s_("tanh"), s_("z_ready")
        convolved, squared = s_("convolved"), s_("squared")
        gates_here, gm_ready = s_("gates_here"), s_("gm_ready")
        k_turned, summed, k_stored, norms = s_("k_turned"), s_("summed"), s_("k_stored"), s_("norms")
        nk_ready = s_("nk_ready")
        v_turned, v_stored = s_("v_turned"), s_("v_stored")
        a_ready, e_ready, e_stored = s_("a_ready"), s_("e_ready"), s_("e_stored")
        att_stored, lt_stored = s_("att_stored"), s_("lt_stored")
        xt_first = [s_(f"xt_first{g}") for g in range(2)]
        mx_ready = [s_(f"mx_ready{g}") for g in range(2)]
        t1_ready = [s_(f"t1_ready{g}") for g in range(2)]
        xmx_ready = [s_(f"xmx_ready{g}") for g in range(2)]
        x_stored = [s_(f"x_stored{g}") for g in range(2)]
        xt_ready = [s_(f"xt_ready{g}") for g in range(2)]
        xt_stored = [s_(f"xt_stored{g}") for g in range(2)]
        ks_ready, qs_ready, r_stored, qs_stored = s_("ks_ready"), s_("qs_ready"), s_("r_stored"), s_("qs_stored")
        us_stored, ds_ready, s_stored = s_("us_stored"), s_("ds_ready"), s_("s_stored")
        u_ready, u_stored, o_ready = s_("u_ready"), s_("u_stored"), s_("o_ready")
        o_stored = s_("o_stored")
        ssq_ready, ms_step, o_scaled, pool_step = s_("ssq_ready"), s_("ms_step"), s_("o_scaled"), s_("pool_step")
        ot_ready, gated_ready, y_ready, y_added = s_("ot_ready"), s_("gated_ready"), s_("y_ready"), s_("y_added")
        LV = len(LEVELS)
        N1 = CH - 1
        INITS = 7
        block = ctx.enter_context(nc.Block())

        def blocks(a, b, odd):
            if len(a.shape) == 2:
                return a.rearrange("p (n two b) -> p n two b", two=2, b=b)[:, :, odd, :]
            return a.rearrange("p u (n two b) -> p u n two b", two=2, b=b)[:, :, :, odd, :]

        def group(a, g):
            return a[:, GU * g:GU * (g + 1)]

        def units(a):
            return a.rearrange("p (u t) -> p u t", u=GU)

        def iterations(eng, body):
            with eng.Fori(0, NK) as hk:
                with eng.Fori(0, B // 2) as bp:
                    for par in range(2):
                        body(hk * B + bp * 2 + par, par, hk, bp)

        def next_head(par, hk, bp):
            return hk if par == 0 else hk + bp

        @block.sync
        def _(sp):
            sp.dma_start(w[:], ins["w_heads"][0]).then_inc(w_loaded, 16)
            with sp.Fori(0, NK - 1) as hk:
                sp.wait_ge(projected, (hk * B + B) * NPJ)
                sp.dma_start(w[:], ins["w_heads"][bass.ds(hk + 1, 1)].rearrange("a p h n -> p (a h) n")).then_inc(w_loaded, 16)
            sp.wait_ge(projected, ITERS * NPJ)
            sp.nop().then_inc(w_loaded, 16)

        @block.tensor
        def _(pe):
            def project(j, col):
                for h in range(CK):
                    last = nc.tensor.matmul(PJ[j % 2][:], w[:, h, j * D:(j + 1) * D], xnT[:, h, bass.ds(col, T)],
                                            start=(h == 0), stop=(h == CK - 1))
                last.then_inc(projected, 1)

            def project_next(it, j, col, loads):
                if j == 0:
                    pe.wait_ge(w_loaded, loads * 16)
                if j < 2:
                    pe.wait_ge(v_stored, it * 2 + j + 1)
                else:
                    pe.wait_ge(copied, ((it + 1) * NCV + j - 1) * 2)
                project(j, col)

            def prepare(it, par):
                c = cv[par]
                pe.wait_ge(convolved, (it * NCV + 1) * 3)
                for n in range(CH):
                    last = nc.tensor.transpose(LOW[0][:, n * P:(n + 1) * P], c[:, KT, n * P:(n + 1) * P], ident[:])
                last.then_inc(k_turned, 1)
                pe.wait_ge(gm_ready, it + 1)
                pe.wait_ge(o_stored, it * CH + 1)
                for g in range(2):
                    nc.tensor.matmul(INV[g][:], tri[:, AFTER, :], group(gm, g).rearrange("p u t -> p (u t)"), start=True, stop=False)
                    nc.tensor.matmul(INV[g][:], eye_b[:], negmask[:], start=False, stop=True).then_inc(e_ready, 1)
                pe.wait_ge(convolved, (it * NCV + 2) * 3)
                for g in range(2):
                    for n in (2 * g, 2 * g + 1):
                        last = nc.tensor.matmul(TRX[g][:, (n % 2) * 2 * P:(n % 2 + 1) * 2 * P].rearrange("p (a t) -> p a t", a=2),
                                                c[:, KT, n * P:(n + 1) * P], c[:, KT:QT + 1, n * P:(n + 1) * P], start=True, stop=True)
                    last.then_inc(a_ready, 1)
                pe.wait_ge(squared, it + 1)
                for n in range(CH):
                    for e in range(2):
                        last = nc.tensor.matmul(LOW[1][:, 2 * n + e:2 * n + e + 1], sq[:, e, n * P:(n + 1) * P], ones1[:],
                                                start=True, stop=True)
                last.then_inc(summed, 1)
                pe.wait_ge(convolved, (it * NCV + NCV) * 3)
                for g in range(2):
                    pe.wait_ge(z_ready, it * HH + g + 1)
                    for n in (2 * g, 2 * g + 1):
                        for e in range(HH):
                            u = HH * (n % 2) + e
                            last = nc.tensor.transpose(PJ[g][:, u * P:(u + 1) * P], c[:, V0 + e, n * P:(n + 1) * P], ident[:])
                    last.then_inc(v_turned, 1)

            def turn_x(g, source):
                for u in range(GU):
                    last = nc.tensor.transpose(TRX[g][:, u * P:(u + 1) * P], source[:, GU * g + u, :], ident[:])
                last.then_inc(xt_ready[g], 1)

            def invert(it, fill):
                for g in range(2):
                    pe.wait_ge(att_stored, it * 2 + g + 1)
                    pe.wait_ge(xt_first[g], it * 2 + 2)
                    turn_x(g, XT)
                for n, b in enumerate(LEVELS):
                    for g in range(2):
                        pe.wait_ge(x_stored[g], it * (LV + 1) + n + 1)
                        for u in range(GU):
                            last = nc.tensor.matmul(INV[g][:, u * HALF:(u + 1) * HALF], Lt[:, GU * g + u, :],
                                                    blocks(X[:, GU * g + u, :], b, 0), start=True, stop=True)
                        last.then_inc(mx_ready[g], 1)
                    fill(2 * n)
                    for g in range(2):
                        pe.wait_ge(t1_ready[g], it * LV + n + 1)
                        if n:
                            pe.wait_ge(xt_stored[g], it * LV + n)
                        for u in range(GU):
                            last = nc.tensor.matmul(INV[g][:, (GU + u) * HALF:(GU + u + 1) * HALF],
                                                    XT[:, GU * g + u, :], T1[:, g, u, :], start=True, stop=True)
                        last.then_inc(xmx_ready[g], 1)
                    fill(2 * n + 1)
                    for g in range(2):
                        pe.wait_ge(x_stored[g], it * (LV + 1) + n + 2)
                        turn_x(g, X)

            def run_chunks(it, par):
                c = cv[par]
                for n in range(CH):
                    k, q = c[:, KT, n * P:(n + 1) * P], c[:, QT, n * P:(n + 1) * P]
                    if n:
                        pe.wait_ge(s_stored, it * N1 + n)
                        nc.tensor.matmul(KS[:, 0:HH * D], k, S[:].rearrange("p e d -> p (e d)"),
                                         start=True, stop=True).then_inc(ks_ready, 1)
                        if n > 1:
                            pe.wait_ge(qs_stored, it * N1 + n - 1)
                        nc.tensor.matmul(QS[:, 0:HH * D], q, S[:].rearrange("p e d -> p (e d)"),
                                         start=True, stop=True).then_inc(qs_ready, 1)
                        pe.wait_ge(r_stored, it * N1 + n)
                    else:
                        for g in range(2):
                            pe.wait_ge(xt_stored[g], it * LV + LV)
                        pe.wait_ge(v_stored, it * 2 + 2)
                    for e in range(HH):
                        last = nc.tensor.matmul(UB[:, e * D:(e + 1) * D], XT[:, HH * n + e, :],
                                                R[:, e, :] if n else vn[:, e, :], start=True, stop=True)
                    last.then_inc(u_ready, 1)
                    if n < N1:
                        if n == 0:
                            pe.wait_ge(y_added, it * 2 + 2)
                        pe.wait_ge(us_stored, it * N1 + n + 1)
                        nc.tensor.matmul(LOW[0][:, 0:HH * D], ktok[:, n, :], us[:].rearrange("p e d -> p (e d)"),
                                         start=True, stop=True).then_inc(ds_ready, 1)
                    pe.wait_ge(u_stored, it * CH + n + 1)
                    if n:
                        pe.wait_ge(o_stored, it * CH + n + 1)
                    for e in range(HH):
                        last = nc.tensor.matmul(OB[:, e * D:(e + 1) * D], attT[:, HH * n + e, :], uh[:, e, :],
                                                start=True, stop=True)
                    last.then_inc(o_ready, 1)

            def turn_outputs(f):
                pe.wait_ge(o_scaled, f + 1)
                for e in range(HH):
                    for n in range(CH):
                        last = nc.tensor.transpose(LOW[e][:, n * P:(n + 1) * P], O[:, HH * n + e, :], ident[:])
                    last.then_inc(ot_ready, 1)

            def project_outputs(f, slot, k):
                if k == 0:
                    pe.wait_ge(gated_ready, f * HH + HH)
                for n in (2 * k, 2 * k + 1):
                    for e in range(HH):
                        last = nc.tensor.matmul(LOW[k][:, (n % 2) * C:(n % 2 + 1) * C], gated[:, e, n * P:(n + 1) * P],
                                                wout[:, bass.ds(slot * (HH * C) + e * C, C)], start=(e == 0), stop=(e == HH - 1))
                last.then_inc(y_ready, 1)

            pe.wait_ge(inits, INITS)
            pe.wait_ge(w_loaded, 16)
            for j in range(NPJ):
                if j >= 2:
                    pe.wait_ge(copied, (j - 1) * 2)
                project(j, 0)

            def body(it, par, hk, bp):
                col = bp * (2 * T) + T if par == 0 else bp * (-2 * T) + 2 * T
                loads = next_head(par, hk, bp) + 1
                slot = hk + bp if par == 0 else hk + 1

                def fill(s):
                    if s % 2 == 0:
                        project_next(it, s // 2, col, loads)
                    elif s == 1:
                        pe.wait_ge(k_stored, it + 1)
                        pe.wait_ge(norms, it * 4 + 1)
                        turn_outputs(it)
                    elif s in (3, 5):
                        project_outputs(it, slot, (s - 3) // 2)
                prepare(it, par)
                invert(it, fill)
                run_chunks(it, par)
            iterations(pe, body)
            turn_outputs(ITERS)
            project_outputs(ITERS, NK, 0)
            project_outputs(ITERS, NK, 1)

        @block.scalar
        def _(act):
            def copy_tile(p, par, j, head):
                act.wait_ge(projected, p * NPJ + j + 1)
                nc.scalar.activation(raw[:, j, TAPS - 1:], PJ[j % 2][:], ACT.Copy).then_inc(copied, 1)
                nc.scalar.activation(cv[par][:, j, :], PJ[j % 2][:], ACT.Copy,
                                     scale=convw[:, bass.ds(head * (NCV * TAPS) + j * TAPS + TAPS - 1, 1)]).then_inc(copied, 1)

            def tanh_tile(p, e):
                act.wait_ge(projected, p * NPJ + NCV + e + 1)
                nc.scalar.activation(zt[:, e, :], PJ[e][:], ACT.Tanh, scale=0.5).then_inc(tanh_done, 1)

            def squares(f):
                act.wait_ge(o_stored, f * CH + 1)
                for u in range(U):
                    last = nc.scalar.activation(junk[:, u, :], O[:, u, :], ACT.Square, accum_out=ssq[:, u:u + 1])
                last.then_inc(ssq_ready, 1)

            act.wait_ge(inits, INITS)
            for j in range(NCV):
                copy_tile(0, 0, j, 0)
            for e in range(HH):
                tanh_tile(0, e)

            def body(it, par, hk, bp):
                for g in range(2):
                    act.wait_ge(e_ready, it * 2 + g + 1)
                    nc.scalar.activation(group(E, g)[:, :, 1:], units(INV[g][:]), ACT.Exp).then_inc(e_stored, 1)
                act.wait_ge(k_turned, it + 1)
                nc.scalar.activation(ktok[:].rearrange("p n d -> p (n d)"), LOW[0][:], ACT.Copy).then_inc(k_stored, 1)
                squares(it)
                for g in range(2):
                    act.wait_ge(xt_ready[g], it * (LV + 1) + 1)
                    nc.scalar.activation(group(X, g), units(TRX[g][:]), ACT.Copy).then_inc(x_stored[g], 1)
                for n, b in enumerate(LEVELS):
                    if n < NCV:
                        act.wait_ge(convolved, (it * NCV + n + 1) * 3)
                        copy_tile(it + 1, 1 - par, n, next_head(par, hk, bp))
                    else:
                        tanh_tile(it + 1, n - NCV)
                    for g in range(2):
                        act.wait_ge(xt_ready[g], it * (LV + 1) + n + 2)
                        nc.scalar.activation(blocks(group(XT, g), b, 1), blocks(units(TRX[g][:]), b, 1),
                                             ACT.Copy).then_inc(xt_stored[g], 1)
                for n in range(CH):
                    if n:
                        act.wait_ge(qs_ready, it * N1 + n)
                        if n > 1:
                            act.wait_ge(o_stored, it * CH + n + 1)
                        for e in range(HH):
                            last = nc.scalar.activation(qss[:, e, :], QS[:, e * D:(e + 1) * D], ACT.Copy,
                                                        scale=gt[par][:, G_INCL, HH * n + e:HH * n + e + 1])
                        last.then_inc(qs_stored, 1)
                    act.wait_ge(u_ready, it * CH + n + 1)
                    if n < N1:
                        act.wait_ge(us_stored, it * N1 + n + 1)
                    nc.scalar.activation(uh[:].rearrange("p e d -> p (e d)"), UB[:, 0:HH * D], ACT.Copy).then_inc(u_stored, 1)
            iterations(act, body)
            squares(ITERS)

        @block.gpsimd
        def _(pool):
            def fetch_gates(it, par):
                nc.gpsimd.tensor_copy(gt[par][:].rearrange("p q u -> p (q u)"), gates[:, bass.ds(it * (NG * U), NG * U)]).then_inc(gates_here, 1)
                pool.wait_ge(gates_here, it + 1)
                nc.gpsimd.tensor_tensor(gm[:], tri[:, UPTO, :].unsqueeze(1).broadcast_to((P, U, P)),
                                        gt[par][:, G_LOG, :].unsqueeze(2).broadcast_to((P, U, P)), ALU.mult).then_inc(gm_ready, 1)

            def squares(p, par):
                pool.wait_ge(convolved, (p * NCV + 2) * 3)
                nc.gpsimd.tensor_tensor(sq[:], cv[par][:, 0:2, :], cv[par][:, 0:2, :], ALU.mult).then_inc(squared, 1)

            def scale_outputs(f):
                pool.wait_ge(ms_step, f * 2 + 2)
                nc.gpsimd.tensor_tensor(rms[:], ms[:], halves[:, 1, :], ALU.pow).then_inc(pool_step, 1)
                pool.wait_ge(pool_step, f + 1)
                nc.gpsimd.tensor_tensor(O[:], O[:], rms[:].unsqueeze(2).broadcast_to((P, U, D)), ALU.mult).then_inc(o_scaled, 1)

            nc.gpsimd.memset(halves[:, 0, :], 0.5).then_inc(inits, 1)
            nc.gpsimd.memset(halves[:, 1, :], -0.5).then_inc(inits, 1)
            pool.wait_ge(inits, INITS)
            fetch_gates(0, 0)
            squares(0, 0)

            def body(it, par, hk, bp):
                pool.wait_ge(norms, it * 4 + 1)
                nc.gpsimd.tensor_tensor(nk[:], n2[par][:, :, 0], halves[:, 0, 0:CH], ALU.pow).then_inc(nk_ready, 1)
                scale_outputs(it)
                pool.wait_ge(e_ready, it * 2 + 2)
                fetch_gates(it + 1, 1 - par)
                pool.wait_ge(summed, it + 1)
                squares(it + 1, 1 - par)
            iterations(pool, body)
            scale_outputs(ITERS)

        @block.vector
        def _(dve):
            def tap(p, par, step, head):
                j, k = step // 3, TAPS - 2 - step % 3
                if step % 3 == 0:
                    dve.wait_ge(copied, (p * NCV + j + 1) * 2)
                else:
                    dve.wait_ge(convolved, p * (NCV * 3) + step)
                nc.vector.scalar_tensor_tensor(cv[par][:, j, :], raw[:, j, k:k + T], convw[:, bass.ds(head * (NCV * TAPS) + j * TAPS + k, 1)],
                                               cv[par][:, j, :], ALU.mult, ALU.add).then_inc(convolved, 1)

            def gate_z(p, par, e):
                dve.wait_ge(tanh_done, p * HH + e + 1)
                nc.vector.scalar_tensor_tensor(zs[par][:, e, :], zt[:, e, :], 1.0, PJ[e][:], ALU.add, ALU.mult).then_inc(z_ready, 1)

            def mean_squares(f, par):
                nc.vector.tensor_scalar(eq[:], n2[par][:, :, 1], RMS_EPS, None, ALU.mult).then_inc(ms_step, 1)
                dve.wait_ge(ms_step, f * 2 + 1)
                dve.wait_ge(ssq_ready, f + 1)
                nc.vector.scalar_tensor_tensor(ms[:].rearrange("p (n e) -> p n e", e=HH), ssq[:].rearrange("p (n e) -> p n e", e=HH), 1.0 / D,
                                               eq[:].unsqueeze(2).broadcast_to((P, CH, HH)), ALU.mult, ALU.add).then_inc(ms_step, 1)

            def gate_outputs(f, par):
                for e in range(HH):
                    dve.wait_ge(ot_ready, f * HH + e + 1)
                    nc.vector.tensor_tensor(gated[:, e, :], LOW[e][:], zs[par][:, e, :], ALU.mult).then_inc(gated_ready, 1)

            def add_y(f, tile, k):
                dve.wait_ge(y_ready, f * 2 + k + 1)
                part = x[:, bass.ds(tile * C + 2 * k * C, 2 * C)]
                nc.vector.tensor_tensor(part, part, LOW[k][:], ALU.add).then_inc(y_added, 1)

            nc.vector.memset(raw[:, :, 0:TAPS - 1], 0.0).then_inc(inits, 1)
            nc.vector.memset(E[:, :, 0:1], 0.0).then_inc(inits, 1)
            nc.vector.memset(n2[1][:], 1.0).then_inc(inits, 1)
            nc.vector.memset(zs[1][:], 0.0).then_inc(inits, 1)
            nc.vector.memset(O[:], 0.0).then_inc(inits, 1)
            dve.wait_ge(inits, INITS)
            nc.vector.nop().then_inc(o_stored, 1)
            for step in range(3 * NCV):
                tap(0, 0, step, 0)
            for e in range(HH):
                gate_z(0, 0, e)

            def body(it, par, hk, bp):
                g_ = gt[par]
                mean_squares(it, 1 - par)
                dve.wait_ge(summed, it + 1)
                nc.vector.tensor_scalar(n2[par][:].rearrange("p n e -> p (n e)"), LOW[1][:, 0:2 * CH], NORM_EPS ** 2, None, ALU.max).then_inc(norms, 1)
                dve.wait_ge(norms, it * 4 + 1)
                nc.vector.reciprocal(rk2[:], n2[par][:, :, 0]).then_inc(norms, 1)
                dve.wait_ge(norms, it * 4 + 2)
                dve.wait_ge(gates_here, it + 1)
                nc.vector.tensor_tensor(cs[:].rearrange("p (n e) -> p n e", e=HH), g_[:, G_BETA, :].rearrange("p (n e) -> p n e", e=HH),
                                        rk2[:].unsqueeze(2).broadcast_to((P, CH, HH)), ALU.mult).then_inc(norms, 1)
                dve.wait_ge(norms, it * 4 + 3)
                nc.vector.tensor_tensor(cr[:], cs[:], g_[:, G_REST, :], ALU.mult).then_inc(norms, 1)
                for g in range(2):
                    dve.wait_ge(a_ready, it * 2 + g + 1)
                    dve.wait_ge(e_stored, it * 2 + g + 1)
                    for u in range(GU * g, GU * (g + 1)):
                        at = (u // HH % 2) * 2 * P
                        last = nc.vector.scalar_tensor_tensor(Lt[:, u, :], TRX[g][:, at:at + P], cs[:, u:u + 1], E[:, u, 0:P],
                                                              ALU.mult, ALU.mult)
                    last.then_inc(lt_stored, 1)
                    for u in range(GU * g, GU * (g + 1)):
                        at = (u // HH % 2) * 2 * P + P
                        last = nc.vector.scalar_tensor_tensor(attT[:, u, :], TRX[g][:, at:at + P], cs[:, u:u + 1], E[:, u, 1:],
                                                              ALU.mult, ALU.mult)
                    last.then_inc(att_stored, 1)
                    dve.wait_ge(lt_stored, it * 2 + g + 1)
                    nc.vector.tensor_tensor(group(XT, g), group(Lt, g), first_mask[:].unsqueeze(1).broadcast_to((P, GU, P)),
                                            ALU.mult).then_inc(xt_first[g], 1)
                    dve.wait_ge(xt_first[g], it * 2 + 1)
                    nc.vector.tensor_tensor(group(XT, g), group(XT, g), ident[:].unsqueeze(1).broadcast_to((P, GU, P)),
                                            ALU.add).then_inc(xt_first[g], 1)
                dve.wait_ge(nk_ready, it + 1)
                for g in range(2):
                    dve.wait_ge(v_turned, it * 2 + g + 1)
                    for n in (2 * g, 2 * g + 1):
                        at = (n % 2) * HH * D
                        last = nc.vector.tensor_scalar(vn[:, HH * n:HH * (n + 1), :].rearrange("p e d -> p (e d)"), PJ[g][:, at:at + HH * D],
                                                       nk[:, n:n + 1], None, ALU.mult)
                    last.then_inc(v_stored, 1)
                head, p = next_head(par, hk, bp), it + 1
                tile = bp * (-2 * CH) + 3 * CH if par == 0 else bp * (2 * CH)

                def fill(s):
                    if s == 2:
                        gate_outputs(it, 1 - par)
                    if s in (5, 6):
                        add_y(it, tile, s - 5)
                    if s >= 2:
                        tap(p, 1 - par, s - 2, head)
                for n, b in enumerate(LEVELS):
                    for g in range(2):
                        dve.wait_ge(mx_ready[g], it * LV + n + 1)
                        nc.vector.tensor_tensor(T1[:, g], INV[g][:, 0:GU * HALF].rearrange("p (u t) -> p u t", u=GU),
                                                lmask[:, n, :].unsqueeze(1).broadcast_to((P, GU, HALF)), ALU.mult).then_inc(t1_ready[g], 1)
                    fill(2 * n)
                    for g in range(2):
                        dve.wait_ge(xmx_ready[g], it * LV + n + 1)
                        xe = blocks(group(X, g), b, 0)
                        nc.vector.tensor_tensor(xe, xe, INV[g][:, GU * HALF:].rearrange("p (u n b) -> p u n b", u=GU, b=b),
                                                ALU.subtract).then_inc(x_stored[g], 1)
                    fill(2 * n + 1)
                for n in range(CH):
                    if n:
                        dve.wait_ge(ks_ready, it * N1 + n)
                        for e in range(HH):
                            u = HH * n + e
                            last = nc.vector.scalar_tensor_tensor(R[:, e, :], KS[:, e * D:(e + 1) * D], g_[:, G_NPREV, u:u + 1],
                                                                  vn[:, u, :], ALU.mult, ALU.add)
                        last.then_inc(r_stored, 1)
                    if n < N1:
                        dve.wait_ge(u_ready, it * CH + n + 1)
                        for e in range(HH):
                            u = HH * n + e
                            last = nc.vector.tensor_scalar(us[:, e, :], UB[:, e * D:(e + 1) * D], cr[:, u:u + 1], None, ALU.mult)
                        last.then_inc(us_stored, 1)
                        dve.wait_ge(ds_ready, it * N1 + n + 1)
                        if n == 0:
                            last = nc.vector.tensor_copy(S[:].rearrange("p e d -> p (e d)"), LOW[0][:, 0:HH * D])
                        else:
                            for e in range(HH):
                                u = HH * n + e
                                last = nc.vector.scalar_tensor_tensor(S[:, e, :], S[:, e, :], g_[:, G_TOTAL, u:u + 1],
                                                                      LOW[0][:, e * D:(e + 1) * D], ALU.mult, ALU.add)
                        last.then_inc(s_stored, 1)
                    dve.wait_ge(o_ready, it * CH + n + 1)
                    o = O[:, HH * n:HH * (n + 1), :].rearrange("p e d -> p (e d)")
                    if n == 0:
                        nc.vector.tensor_copy(o, OB[:, 0:HH * D]).then_inc(o_stored, 1)
                    else:
                        dve.wait_ge(qs_stored, it * N1 + n)
                        nc.vector.tensor_tensor(o, OB[:, 0:HH * D], qss[:].rearrange("p e d -> p (e d)"), ALU.add).then_inc(o_stored, 1)
                    if n < 2:
                        tap(p, 1 - par, 3 * NCV - 2 + n, head)
                    else:
                        gate_z(p, 1 - par, n - 2)
            iterations(dve, body)
            mean_squares(ITERS, (ITERS - 1) % 2)
            gate_outputs(ITERS, (ITERS - 1) % 2)
            for k in range(2):
                add_y(ITERS, CH * (B - 1), k)



SPL_OUT, SPL_COMPRESSION = 1024, 128.9
SPL_N = SPL_OUT * C
SPL_CTRL = max(16, int(SPL_N / SPL_COMPRESSION))
SPL_ROWS = SPL_N // P
SPL_TILES = SPL_ROWS // P
SPL_TAPS = 5
FF1 = SPL_OUT // P
DIM2 = 704
FF2 = -(-DIM2 // P)
ZERO_POINT = 128.0


def spline_constants():
    t = np.linspace(0.0, SPL_CTRL - 1.0, SPL_N, dtype=np.float64)
    i = np.clip(np.floor(t).astype(np.int64), 0, SPL_CTRL - 2)
    f = (t - i).astype(np.float32).astype(np.float64)
    basis = 0.5 * np.stack([-f + 2 * f ** 2 - f ** 3, 2 - 5 * f ** 2 + 3 * f ** 3, f + 4 * f ** 2 - 3 * f ** 3, -f ** 2 + f ** 3])
    first = i[::P]
    step = i - np.repeat(first, P)
    assert step.max() == 1
    weights = np.zeros((SPL_TAPS, SPL_N))
    for k in range(4):
        weights[k + step, np.arange(SPL_N)] = basis[k]
    points = np.clip(first[None, :] - 1 + np.arange(SPL_TAPS)[:, None], 0, SPL_CTRL - 1)
    return points, weights.astype(np.float32)


def spline_weights(nc, sem, banks, keep, ins):
    ident = keep["ident"]
    with ExitStack() as ctx:
        def sb(n, shape, dt=FP32):
            return ctx.enter_context(nc.sbuf_tensor("spl_" + n, shape, dt))
        basis = sb("basis", [P, 2, SPL_TAPS, P])
        points = sb("points", [P, SPL_TILES, 3, SPL_TAPS])
        rows = sb("rows", [P, 2, 3, P])
        loaded, basis_loaded = sem("spl_points_loaded"), [sem(f"spl_basis_loaded{i}") for i in range(2)]
        step, ready, turned, stored = sem("spl_step"), sem("spl_ready"), sem("spl_turned"), sem("spl_stored")
        block = ctx.enter_context(nc.Block())

        @block.sync
        def _(sp):
            sp.dma_start(points[:], ins["spl_points"]).then_inc(loaded, 16)
            for a in range(SPL_TILES):
                if a >= 2:
                    sp.wait_ge(ready, a - 1)
                sp.dma_start(basis[:, a % 2], ins["spl_basis"][a]).then_inc(basis_loaded[a % 2], 16)

        @block.vector
        def _(dve):
            dve.wait_ge(loaded, 16)
            for a in range(SPL_TILES):
                dve.wait_ge(basis_loaded[a % 2], 16 * (a // 2 + 1))
                if a >= 2:
                    dve.wait_ge(turned, a - 1)
                for k in range(SPL_TAPS):
                    if k:
                        dve.wait_ge(step, a * SPL_TAPS + k)
                    for m in range(3):
                        scalar = points[:, a, m, k:k + 1]
                        if k == 0:
                            last = nc.vector.tensor_scalar(rows[:, a % 2, m, :], basis[:, a % 2, k, :], scalar, None, ALU.mult)
                        else:
                            last = nc.vector.scalar_tensor_tensor(rows[:, a % 2, m, :], basis[:, a % 2, k, :], scalar,
                                                                  rows[:, a % 2, m, :], ALU.mult, ALU.add)
                        if m == 2 and k < SPL_TAPS - 1:
                            last.then_inc(step, 1)
                last.then_inc(step, 1)
                dve.wait_ge(step, (a + 1) * SPL_TAPS)
                nc.vector.nop().then_inc(ready, 1)

        @block.tensor
        def _(pe):
            for a in range(SPL_TILES):
                pe.wait_ge(ready, a + 1)
                if a >= 2:
                    pe.wait_ge(stored, 3 * (a - 1))
                for m in range(3):
                    last = nc.tensor.transpose(banks[a % 2][:, m * P:(m + 1) * P], rows[:, a % 2, m, :], ident[:])
                last.then_inc(turned, 1)

        @block.scalar
        def _(act):
            per = P // CK
            for a in range(SPL_TILES):
                act.wait_ge(turned, a + 1)
                for m, dst in enumerate((keep["wg1"], keep["wu1"])):
                    nc.scalar.activation(dst[:].rearrange("p h i -> p i h")[:, a * per:(a + 1) * per, :],
                                         banks[a % 2][:, m * P:(m + 1) * P].rearrange("p (i h) -> p i h", h=CK), ACT.Copy).then_inc(stored, 1)
                cols = P // FF1
                nc.scalar.activation(keep["wd1"][:].rearrange("p i c -> p c i")[:, a * cols:(a + 1) * cols, :],
                                     banks[a % 2][:, 2 * P:3 * P].rearrange("p (c i) -> p c i", i=FF1), ACT.Copy).then_inc(stored, 1)


def norm_phase(nc, sem, banks, keep, name):
    with ExitStack() as ctx:
        v, g, t, s, _ = layer_norm(nc, ctx, sem, name, keep["x"], keep["xnT"], keep["ident"], banks[0:4])
        block = ctx.enter_context(nc.Block())
        block.vector(lambda dve: v(dve))
        block.gpsimd(g)
        block.tensor(t)
        block.scalar(s)


def ffn(nc, sem, banks, keep, name, wg, wu, wd, inner, sg_scale=None, su_scale=None):
    x, xnT = keep["x"], keep["xnT"]
    tiles = inner // P
    with ExitStack() as ctx:
        sg = ctx.enter_context(nc.sbuf_tensor(name + "_sg", [P, 2, T], FP32))
        hid = ctx.enter_context(nc.sbuf_tensor(name + "_hid", [P, 2, T], FP32))
        GATE, UP, Y = banks[0:2], banks[2:4], banks[4:8]
        gate_ready, up_ready, silu_done, hid_ready = (sem(f"{name}_{n}") for n in ("gate", "up", "silu", "hid"))
        down_done, y_ready, y_added = (sem(f"{name}_{n}") for n in ("down", "y", "y_added"))
        block = ctx.enter_context(nc.Block())
        NB = B

        @block.tensor
        def _(pe):
            def gate_up(blk, i, first):
                if not (first and i < 2):
                    pe.wait_ge(silu_done, blk * tiles + i - 1)
                for h in range(CK):
                    last = nc.tensor.matmul(GATE[i % 2][:, :], wg[:, h, i * P:(i + 1) * P], xnT[:, h, bass.ds(blk * T, T)],
                                            start=(h == 0), stop=(h == CK - 1))
                last.then_inc(gate_ready, 1)
                if not (first and i < 2):
                    pe.wait_ge(hid_ready, blk * tiles + i - 1)
                for h in range(CK):
                    last = nc.tensor.matmul(UP[i % 2][:, :], wu[:, h, i * P:(i + 1) * P], xnT[:, h, bass.ds(blk * T, T)],
                                            start=(h == 0), stop=(h == CK - 1))
                last.then_inc(up_ready, 1)

            def down(blk, i, first):
                pe.wait_ge(hid_ready, blk * tiles + i + 1)
                if i == 0 and not first:
                    pe.wait_ge(y_added, blk * CH)
                for n in range(CH):
                    last = nc.tensor.matmul(Y[n][:, 0:C], hid[:, i % 2, n * P:(n + 1) * P], wd[:, i, :],
                                            start=(i == 0), stop=(i == tiles - 1))
                    if i == tiles - 1:
                        last.then_inc(y_ready, 1)
                if i < tiles - 1:
                    last.then_inc(down_done, 1)

            def body(blk, first):
                for i in range(tiles):
                    gate_up(blk, i, first)
                    if i:
                        down(blk, i - 1, first)
                down(blk, tiles - 1, first)
            assert tiles % 2 == 0
            body(0, True)
            with pe.Fori(1, NB) as blk:
                body(blk, False)

        @block.scalar
        def _(act):
            def body(blk, first):
                for i in range(tiles):
                    act.wait_ge(gate_ready, blk * tiles + i + 1)
                    if not (first and i < 2):
                        act.wait_ge(hid_ready, blk * tiles + i - 1)
                    nc.scalar.activation(sg[:, i % 2, :], GATE[i % 2][:, :], ACT.Silu,
                                         scale=1.0 if sg_scale is None else sg_scale[:, i:i + 1]).then_inc(silu_done, 1)
            body(0, True)
            with act.Fori(1, NB) as blk:
                body(blk, False)

        @block.vector
        def _(dve):
            def body(blk, first):
                for i in range(tiles):
                    dve.wait_ge(silu_done, blk * tiles + i + 1)
                    dve.wait_ge(up_ready, blk * tiles + i + 1)
                    if i >= 2:
                        dve.wait_ge(down_done, blk * (tiles - 1) + i - 1)
                    if su_scale is None:
                        last = nc.vector.tensor_tensor(hid[:, i % 2, :], UP[i % 2][:, :], sg[:, i % 2, :], ALU.mult)
                    else:
                        last = nc.vector.scalar_tensor_tensor(hid[:, i % 2, :], UP[i % 2][:, :], su_scale[:, i:i + 1],
                                                              sg[:, i % 2, :], ALU.mult, ALU.mult)
                    last.then_inc(hid_ready, 1)
                for n in range(CH):
                    dve.wait_ge(y_ready, blk * CH + n + 1)
                    part = x[:, bass.ds(blk * (CH * C) + n * C, C)]
                    nc.vector.tensor_tensor(part, part, Y[n][:, 0:C], ALU.add).then_inc(y_added, 1)
            body(0, True)
            with dve.Fori(1, NB) as blk:
                body(blk, False)



KVH, GRP, HD = 8, 4, 8
TH = P // (GRP * HD)
HEADS = TH * GRP
ROPE_BASE = 10000.0
STEP_HEADS = [max(1, T // P // (i + 1)) for i in range(CH)]
STEPS = [(i, s) for i in range(CH) for s in range(HEADS // STEP_HEADS[i])]
SCALE = float(1.0 / np.sqrt(HD))


def attention(nc, sem, banks, keep, ins):
    x, xnT, ident, eye_b = (keep[k] for k in ("x", "xnT", "ident", "eye_b"))
    NS = len(STEPS)
    L1, L2 = 2, 3
    with ExitStack() as ctx:
        def sb(n, shape, dt=FP32):
            return ctx.enter_context(nc.sbuf_tensor("at_" + n, shape, dt))
        w = sb("w", [P, 4, CK, P])
        wv = sb("wv", [P, CK, KVH * HD])
        wo = sb("wo", [P, 2 * C])
        bias = sb("bias", [P, 2, 4])
        bv = sb("bv", [P, KVH * HD])
        bo = sb("bo", [P, C])
        cosines, sines = sb("cosines", [P, T]), sb("sines", [P, T])
        gmask = sb("gmask", [P, GRP])
        cmask = keep["cmask"]
        ta, tb = sb("ta", [P, 2, T]), sb("tb", [P, 2, T])
        qk = sb("qk", [P, 2, T])
        kp = sb("kp", [P, GRP, T])
        v = sb("v", [P, CH, TH * HD])
        mx, nmx = sb("mx", [P, 4, GRP]), sb("nmx", [P, 4, GRP])
        prob = sb("prob", [P, 3, T])
        probT = sb("probT", [P, 3, T])
        rsum, rinv = sb("rsum", [P, CH, HEADS]), sb("rinv", [P, CH, HEADS])
        y, yT = sb("y", [P, P]), sb("yT", [P, P])
        xs = sb("xs", [P, CK, T])
        SC, PT, YB, FB = banks[0:3], banks[3:6], banks[6], banks[7]
        loaded, w_loaded, bo_added = sem("at_loaded"), sem("at_w_loaded"), sem("at_bo_added")
        xs_free, xs_ready = sem("at_xs_free"), sem("at_xs")
        qk_ready, v_ready = sem("at_qk"), sem("at_v")
        rope, qk_done, kp_done, v_done = sem("at_rope"), sem("at_qk_done"), sem("at_kp"), sem("at_v_done")
        s_ready, mx_step, p_ready, pt_ready = sem("at_s"), sem("at_mx"), sem("at_p"), sem("at_pt")
        pt_stored = [sem(f"at_pt_stored{i}") for i in range(2)]
        pv_done = sem("at_pv")
        y_step, yt_ready, yt_stored, out_ready, x_added = (sem("at_" + n) for n in ("y_step", "yt", "yt_stored", "out", "x_added"))
        loads = [(wv[:], ins["at_wv"]), (wo[:], ins["at_wo"]), (bias[:], ins["at_bias"]), (bv[:], ins["at_bv"].partition_broadcast(P)),
                 (bo[:], ins["at_bo"].partition_broadcast(P)), (cosines[:], ins["cosines"]), (sines[:], ins["sines"]),
                 (gmask[:], ins["gmask"])]
        ALL_LOADED = 16 * len(loads)
        assert NS % 2 == 0
        block = ctx.enter_context(nc.Block())

        def iterations(eng, body):
            with eng.Fori(0, 2) as tile:
                with eng.Fori(0, B) as b:
                    body(tile * B + b, tile, b)

        def heads(s):
            i, k = STEPS[s]
            g = STEP_HEADS[i]
            return [(n, (k * g + n) // GRP, (k * g + n) % GRP) for n in range(g)], (i + 1) * P, i

        @block.sync
        def _(sp):
            for dst, src in loads:
                sp.dma_start(dst, src).then_inc(loaded, 16)
            sp.dma_start(w[:], ins["at_w"][0]).then_inc(w_loaded, 16)
            sp.wait_ge(v_ready, B)
            sp.dma_start(w[:], ins["at_w"][1]).then_inc(w_loaded, 16)

        @block.gpsimd
        def _(pool):
            pool.wait_ge(loaded, ALL_LOADED)
            xv = x[:].rearrange("p (t c) -> p t c", c=C)
            nc.gpsimd.tensor_tensor(xv, xv, bo[:].unsqueeze(1).broadcast_to((P, TILES, C)), ALU.add).then_inc(bo_added, 1)

        @block.tensor
        def _(pe):
            def project(it, tile, b):
                pe.wait_ge(w_loaded, tile * 16 + 16)
                for n in range(4):
                    for h in range(CK):
                        last = nc.tensor.matmul(banks[n][:], w[:, n, h, :], xs[:, h, :], start=(h == 0), stop=(h == CK - 1))
                    last.then_inc(qk_ready, 1)
                for n in range(CH):
                    for h in range(CK):
                        last = nc.tensor.matmul(banks[4][:, n * TH * HD:(n + 1) * TH * HD], xs[:, h, n * P:(n + 1) * P],
                                                wv[:, h, bass.ds(tile * (TH * HD), TH * HD)], start=(h == 0), stop=(h == CK - 1))
                last.then_inc(v_ready, 1)

            def scores(it, s):
                hs, n, i = heads(s)
                if s >= 3:
                    pe.wait_ge(p_ready, it * NS + s - 2)
                for k, th, g in hs:
                    rows = slice(GRP * HD * th, GRP * HD * (th + 1))
                    nc.tensor.matmul(SC[s % 3][:, k * n:(k + 1) * n], qk[rows, 0, i * P:(i + 1) * P], kp[rows, g, 0:n],
                                     start=True, stop=False)
                    last = nc.tensor.matmul(SC[s % 3][:, (k + 1) * n - P:(k + 1) * n], eye_b[:], cmask[:], start=False, stop=True)
                last.then_inc(s_ready, 1)

            def turn(it, s):
                hs, n, i = heads(s)
                pe.wait_ge(p_ready, it * NS + s + 1)
                if s >= 3:
                    pe.wait_ge(pt_stored[(s - 3) % 2], it * (NS // 2) + (s - 3) // 2 + 1)
                for k in range(len(hs) * (i + 1)):
                    last = nc.tensor.transpose(PT[s % 3][:, k * P:(k + 1) * P], prob[:, s % 3, k * P:(k + 1) * P], ident[:])
                last.then_inc(pt_ready, 1)

            def times_v(it, s):
                hs, n, i = heads(s)
                pe.wait_ge(pt_stored[s % 2], it * (NS // 2) + s // 2 + 1)
                if i and STEPS[s][1] == 0:
                    pe.wait_ge(y_step, (it * CH + i) * 2)
                for k, th, g in hs:
                    col = (th * GRP + g) * HD
                    for c in range(i + 1):
                        last = nc.tensor.matmul(YB[:, col:col + HD], probT[:, s % 3, k * n + c * P:k * n + (c + 1) * P],
                                                v[:, c, th * HD:(th + 1) * HD], start=(c == 0), stop=(c == i))
                last.then_inc(pv_done, 1)

            def out(it, tile, i):
                pe.wait_ge(y_step, (it * CH + i + 1) * 2)
                if i:
                    pe.wait_ge(x_added, it * CH + i)
                nc.tensor.transpose(FB[:, 0:P], y[:], ident[:]).then_inc(yt_ready, 1)
                pe.wait_ge(yt_stored, it * CH + i + 1)
                nc.tensor.matmul(FB[:, P:P + C], yT[:], wo[:, bass.ds(tile * C, C)], start=True, stop=True).then_inc(out_ready, 1)

            pe.wait_ge(loaded, ALL_LOADED)

            def body(it, tile, b):
                pe.wait_ge(xs_ready, it + 1)
                project(it, tile, b)
                pe.wait_ge(qk_done, it * 2 + 1)
                pe.wait_ge(kp_done, it + 1)
                pe.wait_ge(v_done, it + 1)
                for s in range(NS + L2):
                    if s < NS:
                        scores(it, s)
                    if L1 <= s < NS + L1:
                        turn(it, s - L1)
                    if s >= L2:
                        times_v(it, s - L2)
                        i, k = STEPS[s - L2]
                        if i and k == 1:
                            out(it, tile, i - 1)
                out(it, tile, CH - 1)
                pe.wait_ge(x_added, it * CH + CH)
            iterations(pe, body)

        @block.scalar
        def _(act):
            act.wait_ge(loaded, ALL_LOADED)

            def store(it, s):
                hs, n, i = heads(s)
                act.wait_ge(pt_ready, it * NS + s + 1)
                if s >= 3:
                    act.wait_ge(pv_done, it * NS + s - 2)
                nc.scalar.activation(probT[:, s % 3, 0:len(hs) * n], PT[s % 3][:, 0:len(hs) * n], ACT.Copy).then_inc(pt_stored[0], 1)

            def body(it, tile, b):
                act.wait_ge(xs_free, it + 1)
                nc.scalar.activation(xs[:], xnT[:, :, bass.ds(b * T, T)], ACT.Copy).then_inc(xs_ready, 1)
                for s in range(NS + L1):
                    if s < NS:
                        hs, n, i = heads(s)
                        act.wait_ge(mx_step, (it * NS + s + 1) * 2)
                        if s >= 3:
                            act.wait_ge(pt_ready, it * NS + s - 2)
                        for k, th, g in hs:
                            h = th * GRP + g
                            last = nc.scalar.activation(prob[:, s % 3, k * n:(k + 1) * n], SC[s % 3][:, k * n:(k + 1) * n], ACT.Exp,
                                                        bias=nmx[:, s % 4, k:k + 1], scale=SCALE, accum_out=rsum[:, i, h:h + 1])
                        last.then_inc(p_ready, 1)
                    if s >= L1 and (s - L1) % 2 == 0:
                        store(it, s - L1)
                    if s >= L2 + 1 and STEPS[s - L2 - 1][0] and STEPS[s - L2 - 1][1] == 0:
                        store_y(it, STEPS[s - L2 - 1][0] - 1)
                store_y(it, CH - 1)

            def store_y(it, i):
                act.wait_ge(yt_ready, it * CH + i + 1)
                nc.scalar.activation(yT[:], FB[:, 0:P], ACT.Copy).then_inc(yt_stored, 1)
            iterations(act, body)

        @block.vector
        def _(dve):
            dve.wait_ge(loaded, ALL_LOADED)
            dve.wait_ge(bo_added, 1)
            nc.vector.nop().then_inc(xs_free, 1)

            def body(it, tile, b):
                for n in range(4):
                    dve.wait_ge(qk_ready, it * 4 + n + 1)
                    nc.vector.scalar_tensor_tensor((ta if n % 2 == 0 else tb)[:, n // 2, :], banks[n][:], bias[:, bass.ds(tile, 1), n],
                                                   (cosines if n % 2 == 0 else sines)[:], ALU.add, ALU.mult).then_inc(rope, 1)
                for n in range(2):
                    dve.wait_ge(rope, it * 4 + 2 * n + 2)
                    nc.vector.tensor_tensor(qk[:, n, :], ta[:, n, :], tb[:, n, :], ALU.add).then_inc(qk_done, 1)
                dve.wait_ge(qk_done, it * 2 + 2)
                for g in range(GRP):
                    last = nc.vector.tensor_scalar(kp[:, g, :], qk[:, 1, :], gmask[:, g:g + 1], None, ALU.mult)
                last.then_inc(kp_done, 1)
                dve.wait_ge(v_ready, it + 1)
                nc.vector.tensor_tensor(v[:], banks[4][:, 0:CH * TH * HD].rearrange("p (n d) -> p n d", n=CH),
                                        bv[:, bass.ds(tile * (TH * HD), TH * HD)].unsqueeze(1).broadcast_to((P, CH, TH * HD)),
                                        ALU.add).then_inc(v_done, 1)
                nc.vector.nop().then_inc(xs_free, 1)
                for s in range(NS + L2 + 1):
                    if s < NS:
                        hs, n, i = heads(s)
                        g = len(hs)
                        dve.wait_ge(s_ready, it * NS + s + 1)
                        nc.vector.tensor_reduce(mx[:, s % 4, 0:g], SC[s % 3][:, 0:g * n].rearrange("p (g n) -> p g n", g=g),
                                                AX.X, ALU.max).then_inc(mx_step, 1)
                        dve.wait_ge(mx_step, (it * NS + s) * 2 + 1)
                        nc.vector.tensor_scalar(nmx[:, s % 4, 0:g], mx[:, s % 4, 0:g], -SCALE, None, ALU.mult).then_inc(mx_step, 1)
                    if L1 <= s < NS + L1 and (s - L1) % 2 == 1:
                        t_ = s - L1
                        hs, n, i = heads(t_)
                        dve.wait_ge(pt_ready, it * NS + t_ + 1)
                        if t_ >= 3:
                            dve.wait_ge(pv_done, it * NS + t_ - 2)
                        nc.vector.tensor_copy(probT[:, t_ % 3, 0:len(hs) * n], PT[t_ % 3][:, 0:len(hs) * n]).then_inc(pt_stored[1], 1)
                    k = s - L2
                    if k == NS or (k > 0 and STEPS[k][1] == 0):
                        normalise(it, STEPS[k - 1][0], k)
                    if k > 2 and k - 2 < NS and STEPS[k - 2][1] == 0 and STEPS[k - 2][0]:
                        add(it, b, STEPS[k - 2][0] - 1)
                add(it, b, CH - 1)

            def normalise(it, i, k):
                dve.wait_ge(pv_done, it * NS + k)
                nc.vector.reciprocal(rinv[:, i, :], rsum[:, i, :]).then_inc(y_step, 1)
                dve.wait_ge(y_step, (it * CH + i) * 2 + 1)
                nc.vector.tensor_tensor(y[:].rearrange("p (h d) -> p h d", d=HD), YB[:, 0:P].rearrange("p (h d) -> p h d", d=HD),
                                        rinv[:, i, :].unsqueeze(2).broadcast_to((P, HEADS, HD)), ALU.mult).then_inc(y_step, 1)

            def add(it, b, i):
                dve.wait_ge(out_ready, it * CH + i + 1)
                part = x[:, bass.ds(b * (CH * C) + i * C, C)]
                nc.vector.tensor_tensor(part, part, FB[:, P:P + C], ALU.add).then_inc(x_added, 1)
            iterations(dve, body)


def dequantise(nc, sem, keep, ins):
    with ExitStack() as ctx:
        def sb(n, shape, dt=FP32):
            return ctx.enter_context(nc.sbuf_tensor("dq_" + n, shape, dt))
        qg, qu, qd = sb("qg", [P, CK, FF2 * P], INT32), sb("qu", [P, CK, FF2 * P], INT32), sb("qd", [P, FF2, C], INT32)
        sd = sb("sd", [P, C])
        loaded, step = sem("dq_loaded"), sem("dq_step")
        block = ctx.enter_context(nc.Block())

        @block.sync
        def _(sp):
            for dst, src in ((qg[:], ins["q_gate"]), (qu[:], ins["q_up"]), (sd[:], ins["s_down"].partition_broadcast(P)),
                             (qd[:], ins["q_down"]), (keep["s_gate"][:], ins["s_gate"]), (keep["s_up"][:], ins["s_up"])):
                sp.dma_start(dst, src).then_inc(loaded, 16)

        @block.vector
        def _(dve):
            dve.wait_ge(loaded, 16 * 6)
            nc.vector.tensor_scalar(keep["wg2"][:], qg[:], -ZERO_POINT, None, ALU.add)
            nc.vector.tensor_scalar(keep["wu2"][:], qu[:], -ZERO_POINT, None, ALU.add)
            nc.vector.tensor_scalar(keep["wd2"][:], qd[:], -ZERO_POINT, None, ALU.add).then_inc(step, 1)
            dve.wait_ge(step, 1)
            nc.vector.tensor_tensor(keep["wd2"][:], keep["wd2"][:], sd[:].unsqueeze(1).broadcast_to((P, FF2, C)), ALU.mult)


class Semaphores:
    def __init__(self, nc, ctx):
        self.nc, self.ctx, self.found = nc, ctx, {}

    def __call__(self, name):
        if name not in self.found:
            self.found[name] = self.ctx.enter_context(self.nc.semaphore(name))
        return self.found[name]


def program(nc, ins, out):
    with ExitStack() as ctx:
        sem = Semaphores(nc, ctx)
        banks = [ctx.enter_context(nc.psum_tensor(f"bank{i}", [P, 512], FP32)) for i in range(8)]

        def sb(stack, n, shape, dt=FP32):
            return stack.enter_context(nc.sbuf_tensor(n, shape, dt))
        keep = {"x": sb(ctx, "x", [P, TILES * C]), "xnT": sb(ctx, "xnT", [P, CK, B * T]), "ident": sb(ctx, "ident", [P, P]),
                "ones1": sb(ctx, "ones1", [P, 1]), "eye_b": sb(ctx, "eye_b", [P, P], BF16), "cmask": sb(ctx, "cmask", [P, P], BF16)}
        with ExitStack() as first:
            keep["gates"] = sb(first, "gates", [P, (ITERS + 1) * NG * U])
            keep["wout"] = sb(first, "wout", [P, (NK + 1) * HH * C])
            keep["convw"] = sb(first, "convw", [P, (NK + 1) * NCV * TAPS])
            keep["tri"] = sb(first, "tri", [P, 4, P])
            keep["negmask"] = sb(first, "negmask", [P, GU * P], BF16)
            keep["first_mask"] = sb(first, "first_mask", [P, P])
            keep["lmask"] = sb(first, "lmask", [P, len(LEVELS), HALF])
            first_norm_and_gates(nc, sem, banks, keep, ins)
            delta_rule(nc, sem, banks, keep, ins)
        with ExitStack() as second:
            for name in ("wg1", "wu1"):
                keep[name] = sb(second, name, [P, CK, SPL_OUT])
            keep["wd1"] = sb(second, "wd1", [P, FF1, C])
            spline_weights(nc, sem, banks, keep, ins)
            norm_phase(nc, sem, banks, keep, "ln2")
            ffn(nc, sem, banks, keep, "ff1", keep["wg1"], keep["wu1"], keep["wd1"], SPL_OUT)
        norm_phase(nc, sem, banks, keep, "ln3")
        attention(nc, sem, banks, keep, ins)
        with ExitStack() as third:
            for name in ("wg2", "wu2"):
                keep[name] = sb(third, name, [P, CK, FF2 * P])
            keep["wd2"] = sb(third, "wd2", [P, FF2, C])
            keep["s_gate"], keep["s_up"] = sb(third, "s_gate", [P, FF2]), sb(third, "s_up", [P, FF2])
            dequantise(nc, sem, keep, ins)
            norm_phase(nc, sem, banks, keep, "ln4")
            ffn(nc, sem, banks, keep, "ff2", keep["wg2"], keep["wu2"], keep["wd2"], FF2 * P, keep["s_gate"], keep["s_up"])
        x = keep["x"]
        written = sem("written")
        block = ctx.enter_context(nc.Block())

        @block.sync
        def _(sp):
            for b in range(B):
                sp.dma_start(out[b * T:(b + 1) * T, :].rearrange("(j p) c -> p j c", p=P),
                             x[:, CH * b * C:CH * (b + 1) * C].rearrange("p (j c) -> p j c", c=C)).then_inc(written, 16)
            sp.wait_ge(written, 16 * B)


def layouts(d):
    f = lambda a: np.ascontiguousarray(a)
    r = np.arange(P)
    h = {}
    h["x"] = f(d["L0_attn_x"]).reshape(B * T, C)

    def by_channel(w):
        return w.T.reshape(CK, P, -1).transpose(1, 0, 2)
    wqkv, wz = d["L0_attn_W_qkv"], d["L0_attn_W_z"]
    heads = []
    conv = []
    for k in range(NK):
        q, kk = slice(k * D, (k + 1) * D), slice(NK * D + k * D, NK * D + (k + 1) * D)
        v = slice(2 * NK * D + HH * k * D, 2 * NK * D + HH * (k + 1) * D)
        z = slice(HH * k * D, HH * (k + 1) * D)
        heads.append(by_channel(np.concatenate([wqkv[kk], wqkv[q], wqkv[v], wz[z]])))
        cw = d["L0_attn_conv_w"]
        conv.append(np.concatenate([cw[kk], cw[q], cw[v]]).reshape(NCV, P, TAPS).transpose(1, 0, 2))
    h["w_heads"] = f(np.stack(heads))
    h["conv_w"] = f(np.stack(conv, 1)).reshape(P, NK * NCV * TAPS)
    h["w_ab"] = f(by_channel(np.concatenate([d["L0_attn_W_b"], d["L0_attn_W_a"]])))
    h["dt_bias"], h["A_log"] = f(d["L0_attn_dt_bias"]), f(d["L0_attn_A_log"])
    h["norm_w"] = f(d["L0_attn_norm_w"]).reshape(P, 1)
    h["w_out"] = f(d["L0_attn_W_out"].T.reshape(NV, D, C).transpose(1, 0, 2)).reshape(P, NV * C)
    j, t = r[:, None], r[None, :]
    h["ident"] = np.eye(P, dtype=np.float32)
    h["tri"] = f(np.stack([j <= t, j < t, j > t, j >= 0 * t], 1).astype(np.float32))
    h["first_mask"] = f(-((t % 2 == 1) & (j == t - 1)).astype(np.float32))
    col = np.arange(HALF)
    h["lmask"] = f(np.stack([(j // b == 2 * (col // b)[None, :] + 1) for b in LEVELS], 1).astype(np.float32))
    points, basis = spline_constants()
    cps = np.stack([d[f"L0_ffn_{n}_cp"][points] for n in ("gate", "up", "down")])
    h["spl_points"] = f(cps.reshape(3, SPL_TAPS, SPL_TILES, P).transpose(3, 2, 0, 1))
    h["spl_basis"] = f(basis.reshape(SPL_TAPS, SPL_TILES, P, P).transpose(1, 2, 0, 3))
    row = np.arange(2 * P)
    kv = row // (GRP * HD) * HD + row % HD
    turn = lambda c: c // HD * HD + (c % HD + HD // 2) % HD
    q, k = d["L1_attn_Wq"], d["L1_attn_Wk"]
    four = [q, q[turn(row)], k[kv], k[turn(kv)]]
    h["at_w"] = f(np.stack([np.stack([by_channel(a[t_ * P:(t_ + 1) * P]) for a in four], 1) for t_ in range(2)]))
    bq, bk = d["L1_attn_bq"], d["L1_attn_bk"]
    h["at_bias"] = f(np.stack([bq, bq[turn(row)], bk[kv], bk[turn(kv)]], -1).reshape(2, P, 4).transpose(1, 0, 2))
    h["at_wv"] = f(by_channel(d["L1_attn_Wv"]))
    h["at_bv"], h["at_bo"] = f(d["L1_attn_bv"]), f(d["L1_attn_bo"])
    h["at_wo"] = f(d["L1_attn_Wo"].T.reshape(2, P, C).transpose(1, 0, 2)).reshape(P, 2 * C)
    jj = (r % HD % (HD // 2)).astype(np.float32)
    theta = np.float32(ROPE_BASE) ** (np.float32(-2.0) * jj / np.float32(HD))
    ang = (np.arange(T, dtype=np.float32) + 1.0)[None, :] * theta.astype(np.float32)[:, None]
    h["cosines"] = f(np.cos(ang.astype(np.float64)).astype(np.float32))
    sign = np.where(r % HD < HD // 2, -1.0, 1.0)[:, None]
    h["sines"] = f((sign * np.sin(ang.astype(np.float64))).astype(np.float32))
    h["gmask"] = f(((r % (GRP * HD)) // HD == np.arange(GRP)[:, None]).T.astype(np.float32))

    def padded(a):
        return np.concatenate([a, np.zeros((FF2 * P - DIM2, *a.shape[1:]), a.dtype)])
    h["q_gate"], h["q_up"] = f(by_channel(padded(d["L1_ffn_wq_gate"]))), f(by_channel(padded(d["L1_ffn_wq_up"])))

    def inner_tiles(a):
        return f(np.moveaxis(padded(a).reshape(FF2, P, *a.shape[1:]), 0, 1))
    h["q_down"] = inner_tiles(d["L1_ffn_wq_down"].T)
    h["s_gate"], h["s_up"], h["s_down"] = inner_tiles(d["L1_ffn_s_gate"]), inner_tiles(d["L1_ffn_s_up"]), f(d["L1_ffn_s_down"])
    return h


def kernel(**inputs):
    import concourse.bacc as bacc
    from concourse.bass_utils import run_bass_kernel_spmd
    nc = bacc.Bacc("TRN2", target_bir_lowering=False, num_devices=1)
    arrays, ins = {}, {}
    for name, a in layouts({k: np.asarray(v) for k, v in inputs.items()}).items():
        arrays[f"in_{name}"] = a
        ins[name] = nc.dram_tensor(f"in_{name}", a.shape, mybir.dt.from_np(a.dtype), kind="ExternalInput").ap()
    out = nc.dram_tensor("out_y", (B * T, C), FP32, kind="ExternalOutput").ap()
    program(nc, ins, out)
    r = run_bass_kernel_spmd(nc, [arrays], core_ids=[0])
    return r.results[0]["out_y"].reshape(B, T, C)
```

```python
from contextlib import ExitStack

import numpy as np

import concourse.bass as bass
from concourse import mybir

FP32 = mybir.dt.float32
BF16 = mybir.dt.bfloat16
INT32 = mybir.dt.int32
ALU = mybir.AluOpType
ACT = mybir.ActivationFunctionType
AX = mybir.AxisListType

P = 128
B, T, C = 4, 512, 256
TILES = B * T // P
CH = T // P
CK = C // P
NK, NV, D = 16, 32, 128
HH = NV // NK
TAPS = 4
U = CH * HH
GU = U // 2
LEVELS = [2, 4, 8, 16, 32, 64]
HALF = P // 2
ITERS = NK * B
KT, QT, V0 = 0, 1, 2
NCV, NPJ = 4, 6
LN_EPS, RMS_EPS, NORM_EPS = 1e-5, 1e-6, 1e-12

G_LOG, G_NPREV, G_INCL, G_REST, G_BETA, G_TOTAL = range(6)
NG = 6
UPTO, BEFORE, AFTER, ALL = range(4)


def layer_norm(nc, ctx, sem, name, x, xnT, ident, banks):
    def sb(n, shape):
        return ctx.enter_context(nc.sbuf_tensor(f"{name}_{n}", shape, FP32))
    stats = sb("stats", [P, 2, CH, 6])
    mv = sb("mv", [P, 2, CH, 2])
    ve = sb("ve", [P, 2, CH])
    rstd = sb("rstd", [P, 2, CH])
    xn = sb("xn", [P, 2, CH, C])
    half = sb("neghalf", [P, CH])
    stats_done, var_ready, rstd_ready = sem(name + "_stats"), sem(name + "_var"), sem(name + "_rstd")
    xn_ready, turned, stored, const = sem(name + "_xn"), sem(name + "_turned"), sem(name + "_stored"), sem(name + "_const")

    def vector(dve, before=lambda b: None):
        def statistics(b):
            before(b)
            for j in range(CH):
                last = nc.vector.bn_stats(stats[:, b % 2, j, :], x[:, (CH * b + j) * C:(CH * b + j + 1) * C])
            last.then_inc(stats_done, 1)
            dve.wait_ge(stats_done, 2 * b + 1)
            for j in range(CH):
                last = nc.vector.bn_aggr(mv[:, b % 2, j, :], stats[:, b % 2, j, :])
            last.then_inc(stats_done, 1)
            dve.wait_ge(stats_done, 2 * b + 2)
            nc.vector.tensor_scalar(ve[:, b % 2, :], mv[:, b % 2, :, 1], LN_EPS, None, ALU.add).then_inc(var_ready, 1)

        def normalise(b):
            dve.wait_ge(rstd_ready, b + 1)
            if b >= 2:
                dve.wait_ge(turned, b - 1)
            for j in range(CH):
                last = nc.vector.tensor_scalar(xn[:, b % 2, j, :], x[:, (CH * b + j) * C:(CH * b + j + 1) * C], mv[:, b % 2, j, 0:1],
                                               rstd[:, b % 2, j:j + 1], ALU.subtract, ALU.mult)
            last.then_inc(xn_ready, 1)
        statistics(0)
        for b in range(B):
            if b + 1 < B:
                statistics(b + 1)
            normalise(b)

    def gpsimd(pool):
        nc.gpsimd.memset(half[:], -0.5).then_inc(const, 1)
        pool.wait_ge(const, 1)
        for b in range(B):
            pool.wait_ge(var_ready, b + 1)
            if b >= 2:
                pool.wait_ge(xn_ready, b - 1)
            nc.gpsimd.tensor_tensor(rstd[:, b % 2, :], ve[:, b % 2, :], half[:], ALU.pow).then_inc(rstd_ready, 1)

    def tensor(pe):
        for b in range(B):
            pe.wait_ge(xn_ready, b + 1)
            if b >= 2:
                pe.wait_ge(stored, CK * (b - 1))
            for h in range(CK):
                for j in range(CH):
                    last = nc.tensor.transpose(banks[2 * (b % 2) + h][:, j * P:(j + 1) * P],
                                               xn[:, b % 2, j, h * P:(h + 1) * P], ident[:])
            last.then_inc(turned, 1)

    def scalar(act):
        for b in range(B):
            act.wait_ge(turned, b + 1)
            for h in range(CK):
                nc.scalar.activation(xnT[:, h, b * T:(b + 1) * T], banks[2 * (b % 2) + h][:], ACT.Copy).then_inc(stored, 1)

    return vector, gpsimd, tensor, scalar, stored


def first_norm_and_gates(nc, sem, banks, keep, ins):
    x, xnT, gates, wout, ident, convw = (keep[k] for k in ("x", "xnT", "gates", "wout", "ident", "convw"))
    tri, ones1 = keep["tri"], keep["ones1"]
    with ExitStack() as ctx:
        def sb(n, shape, dt=FP32):
            return ctx.enter_context(nc.sbuf_tensor("p1_" + n, shape, dt))
        N = ITERS * U
        wab = sb("wab", [P, CK, 2 * NV])
        dtb = sb("dtb", [P, NV])
        expa = sb("expa", [P, NV])
        normw = sb("normw", [P, 1])
        nb, na, ga, lg, mx = (sb(n, [P, N]) for n in ("nb", "na", "ga", "lg", "mx"))
        loaded, x_loaded = sem("p1_loaded"), sem("p1_x_loaded")
        act_step, dve_step, pe_step = sem("p1_act"), sem("p1_dve"), sem("p1_pe")
        v, g, t, s, stored = layer_norm(nc, ctx, sem, "ln1", x, xnT, ident, banks[0:4])
        loads = [(ident[:], ins["ident"]), (wab[:], ins["w_ab"]), (convw[:, 0:NK * NCV * TAPS], ins["conv_w"]), (tri[:], ins["tri"]),
                 (keep["lmask"][:], ins["lmask"]),
                 (keep["first"][:], ins["first"]), (keep["odd"][:], ins["odd"]), (normw[:], ins["norm_w"]), (dtb[:], ins["dt_bias"].partition_broadcast(P)),
                 (expa[:], ins["A_log"].partition_broadcast(P)), (wout[:, HH * C:], ins["w_out"])]
        ALL_LOADED = 16 * len(loads)

        def by_head(a):
            return a.rearrange("p (k t e) -> p k t e", k=NK, e=HH)

        def quantity(q):
            return gates[:, 0:ITERS * NG * U].rearrange("p (i q u) -> p i q u", q=NG, u=U)[:, :, q, :]

        def flat(a):
            return a.rearrange("p (i u) -> p i u", u=U)
        block = ctx.enter_context(nc.Block())

        @block.sync
        def _(sp):
            for b in range(B):
                sp.dma_start(x[:, CH * b * C:CH * (b + 1) * C].rearrange("p (j c) -> p j c", c=C),
                             ins["x"][b * T:(b + 1) * T, :].rearrange("(j p) c -> p j c", p=P)).then_inc(x_loaded, 16)

        @block.scalar
        def _(act):
            for dst, src in loads:
                act.dma_start(dst, src).then_inc(loaded, 16)
            s(act)
            act.wait_ge(dve_step, 1)
            nc.scalar.activation(nb[:], nb[:], ACT.Exp, scale=-1.0).then_inc(act_step, 1)
            act.wait_ge(loaded, ALL_LOADED)
            nc.scalar.activation(expa[:], expa[:], ACT.Exp).then_inc(act_step, 1)
            act.wait_ge(dve_step, 2)
            nc.scalar.activation(ga[:], na[:], ACT.Abs).then_inc(act_step, 1)
            act.wait_ge(act_step, 3)
            nc.scalar.activation(ga[:], ga[:], ACT.Exp, scale=-1.0).then_inc(act_step, 1)
            act.wait_ge(act_step, 4)
            nc.scalar.activation(ga[:], ga[:], ACT.Ln, bias=1.0).then_inc(act_step, 1)
            for n, q in enumerate((G_NPREV, G_INCL, G_REST, G_TOTAL)):
                act.wait_ge(pe_step, 2 + n)
                nc.scalar.activation(quantity(q), flat(banks[4 + n][:]), ACT.Exp).then_inc(act_step, 1)

        @block.gpsimd
        def _(pool):
            nc.gpsimd.memset(ones1[:], 1.0)
            nc.gpsimd.memset(convw[:, NK * NCV * TAPS:], 0.0)
            nc.gpsimd.memset(gates[:, ITERS * NG * U:], 0.0)
            nc.gpsimd.memset(wout[:, 0:HH * C], 0.0)
            g(pool)

        @block.tensor
        def _(pe):
            pe.wait_ge(loaded, ALL_LOADED)
            t(pe)
            pe.wait_ge(stored, CK * B)
            for tt in range(TILES):
                for h in range(CK):
                    last = nc.tensor.matmul(banks[4 + tt // 8][:, (tt % 8) * 2 * NV:(tt % 8 + 1) * 2 * NV],
                                            xnT[:, h, tt * P:(tt + 1) * P], wab[:, h, :], start=(h == 0), stop=(h == CK - 1))
            last.then_inc(pe_step, 1)
            pe.wait_ge(dve_step, 5)
            for n, w in enumerate((BEFORE, UPTO, AFTER, ALL)):
                nc.tensor.matmul(banks[4 + n][:], tri[:, w, :], lg[:], start=True, stop=True).then_inc(pe_step, 1)

        @block.vector
        def _(dve):
            v(dve, lambda b: dve.wait_ge(x_loaded, 16 * B))
            dve.wait_ge(loaded, ALL_LOADED)
            dve.wait_ge(pe_step, 1)
            for n, dst in enumerate((nb, na)):
                for k in range(2):
                    last = nc.vector.tensor_copy(by_head(dst[:])[:, :, 8 * k:8 * k + 8, :],
                                                 banks[4 + k][:].rearrange("p (t w k e) -> p w k t e", w=2, k=NK, e=HH)[:, n])
            last.then_inc(dve_step, 1)
            dve.wait_ge(dve_step, 1)
            nc.vector.tensor_tensor(by_head(na[:]), by_head(na[:]),
                                    dtb[:].rearrange("p (k e) -> p k e", e=HH).unsqueeze(2).broadcast_to((P, NK, TILES, HH)),
                                    ALU.add).then_inc(dve_step, 1)
            dve.wait_ge(dve_step, 2)
            nc.vector.tensor_scalar(mx[:], na[:], 0.0, None, ALU.max).then_inc(dve_step, 1)
            dve.wait_ge(act_step, 5)
            dve.wait_ge(dve_step, 3)
            nc.vector.scalar_tensor_tensor(mx[:], mx[:], -1.0, ga[:], ALU.mult, ALU.subtract).then_inc(dve_step, 1)
            dve.wait_ge(dve_step, 4)
            nc.vector.tensor_tensor(by_head(lg[:]), by_head(mx[:]),
                                    expa[:].rearrange("p (k e) -> p k e", e=HH).unsqueeze(2).broadcast_to((P, NK, TILES, HH)),
                                    ALU.mult).then_inc(dve_step, 1)
            dve.wait_ge(dve_step, 5)
            nc.vector.tensor_copy(quantity(G_LOG), flat(lg[:]))
            nc.vector.tensor_copy(keep["eye_b"][:], ident[:])
            nc.vector.tensor_scalar(keep["negmask"][:].rearrange("p (u t) -> p u t", u=GU), tri[:, AFTER, :].unsqueeze(1).broadcast_to((P, GU, P)),
                                    -30000.0, None, ALU.mult)
            nc.vector.tensor_scalar(keep["cmask"][:], tri[:, BEFORE, :], -1e30, None, ALU.mult)
            nc.vector.tensor_scalar(nb[:], nb[:], 1.0, None, ALU.add).then_inc(dve_step, 1)
            dve.wait_ge(dve_step, 6)
            nc.vector.reciprocal(quantity(G_BETA), flat(nb[:]))
            nc.vector.tensor_scalar(wout[:, HH * C:], wout[:, HH * C:], normw[:, 0:1], 0.5, ALU.mult, ALU.mult)
            dve.wait_ge(act_step, 9)
            nc.vector.tensor_scalar(quantity(G_NPREV), quantity(G_NPREV), -1.0, None, ALU.mult)


def delta_rule(nc, sem, banks, keep, ins):
    x, xnT, gates, wout, ident, convw = (keep[k] for k in ("x", "xnT", "gates", "wout", "ident", "convw"))
    tri, negmask, eye_b, first, odd, lmask, ones1 = (keep[k] for k in ("tri", "negmask", "eye_b", "first", "odd", "lmask", "ones1"))
    with ExitStack() as ctx:
        def sb(n, shape, dt=FP32):
            return ctx.enter_context(nc.sbuf_tensor("gd_" + n, shape, dt))
        w = sb("w", [P, CK, NPJ * D])
        raw = sb("raw", [P, NCV, TAPS - 1 + T])
        cv = [sb(f"cv{i}", [P, NCV, T]) for i in range(2)]
        zs = [sb(f"zs{i}", [P, HH, T]) for i in range(2)]
        zt = sb("zt", [P, HH, T])
        sq = sb("sq", [P, 2, T])
        gt = [sb(f"gt{i}", [P, NG, U]) for i in range(2)]
        gm = sb("gm", [P, U, P])
        n2 = [sb(f"n2{i}", [P, CH, 2]) for i in range(2)]
        nk = sb("nk", [P, CH])
        rk2 = sb("rk2", [P, CH])
        cs = sb("cs", [P, U])
        cr = sb("cr", [P, U])
        halves = sb("halves", [P, 2, U])
        ktok = sb("ktok", [P, CH, D])
        vn = sb("vn", [P, U, D])
        E = sb("E", [P, U, 1 + P])
        Lt = sb("Lt", [P, U, P])
        attT = sb("attT", [P, U, P])
        X = sb("X", [P, U, P])
        XT = sb("XT", [P, U, P])
        T1 = sb("T1", [P, 2, GU, HALF])
        S = sb("S", [P, HH, D])
        R = sb("R", [P, HH, D])
        uh = sb("uh", [P, HH, D])
        us = sb("us", [P, HH, D])
        qss = sb("qss", [P, HH, D])
        O = sb("O", [P, U, D])
        junk = sb("junk", [P, U, D])
        ssq = sb("ssq", [P, U])
        eq = sb("eq", [P, CH])
        ms = sb("ms", [P, U])
        rms = sb("rms", [P, U])
        gated = sb("gated", [P, HH, T])
        PJ = [banks[0], banks[1]]
        INV = [banks[2], banks[3]]
        TRX = [banks[4], banks[5]]
        KS, QS, UB, OB = banks[2:6]
        LOW = [banks[6], banks[7]]

        s_ = lambda n: sem("gd_" + n)
        inits = s_("inits")
        w_loaded = s_("w_loaded")
        projected, copied = s_("projected"), s_("copied")
        tanh_done, z_ready = s_("tanh"), s_("z_ready")
        convolved, squared = s_("convolved"), s_("squared")
        gates_here, gm_ready = s_("gates_here"), s_("gm_ready")
        xt_init = s_("xt_init")
        k_turned, summed, k_stored, norms = s_("k_turned"), s_("summed"), s_("k_stored"), s_("norms")
        nk_ready = s_("nk_ready")
        v_turned, v_stored = s_("v_turned"), s_("v_stored")
        a_ready, e_ready, e_stored = s_("a_ready"), s_("e_ready"), s_("e_stored")
        att_stored, lt_stored = s_("att_stored"), s_("lt_stored")
        xt_first = [s_(f"xt_first{g}") for g in range(2)]
        mx_ready = [s_(f"mx_ready{g}") for g in range(2)]
        t1_ready = [s_(f"t1_ready{g}") for g in range(2)]
        xmx_ready = [s_(f"xmx_ready{g}") for g in range(2)]
        x_stored = [s_(f"x_stored{g}") for g in range(2)]
        xt_ready = [s_(f"xt_ready{g}") for g in range(2)]
        xt_stored = [s_(f"xt_stored{g}") for g in range(2)]
        ks_ready, qs_ready, r_stored, qs_stored = s_("ks_ready"), s_("qs_ready"), s_("r_stored"), s_("qs_stored")
        us_stored, ds_ready, s_stored = s_("us_stored"), s_("ds_ready"), s_("s_stored")
        u_ready, u_stored, o_ready = s_("u_ready"), s_("u_stored"), s_("o_ready")
        o_stored = s_("o_stored")
        ssq_ready, ms_step, o_scaled, pool_step = s_("ssq_ready"), s_("ms_step"), s_("o_scaled"), s_("pool_step")
        ot_ready, gated_ready, y_ready, y_added = s_("ot_ready"), s_("gated_ready"), s_("y_ready"), s_("y_added")
        LV = len(LEVELS)
        N1 = CH - 1
        INITS = 7
        block = ctx.enter_context(nc.Block())

        def blocks(a, b, odd):
            if len(a.shape) == 2:
                return a.rearrange("p (n two b) -> p n two b", two=2, b=b)[:, :, odd, :]
            return a.rearrange("p u (n two b) -> p u n two b", two=2, b=b)[:, :, :, odd, :]

        def columns(a, odd_ones):
            if len(a.shape) == 2:
                return a.rearrange("p (n two) -> p n two", two=2)[:, :, odd_ones]
            return a.rearrange("p u (n two) -> p u n two", two=2)[:, :, :, odd_ones]

        def group(a, g):
            return a[:, GU * g:GU * (g + 1)]

        def units(a):
            return a.rearrange("p (u t) -> p u t", u=GU)

        def iterations(eng, body):
            with eng.Fori(0, NK) as hk:
                with eng.Fori(0, B // 2) as bp:
                    for par in range(2):
                        body(hk * B + bp * 2 + par, par, hk, bp)

        def next_head(par, hk, bp):
            return hk if par == 0 else hk + bp

        @block.sync
        def _(sp):
            sp.dma_start(w[:], ins["w_heads"][0]).then_inc(w_loaded, 16)
            with sp.Fori(0, NK - 1) as hk:
                sp.wait_ge(projected, (hk * B + B) * NPJ)
                sp.dma_start(w[:], ins["w_heads"][bass.ds(hk + 1, 1)].rearrange("a p h n -> p (a h) n")).then_inc(w_loaded, 16)
            sp.wait_ge(projected, ITERS * NPJ)
            sp.nop().then_inc(w_loaded, 16)

        @block.tensor
        def _(pe):
            def project(j, col, halves=range(CK)):
                for h in halves:
                    last = nc.tensor.matmul(PJ[j % 2][:], w[:, h, j * D:(j + 1) * D], xnT[:, h, bass.ds(col, T)],
                                            start=(h == 0), stop=(h == CK - 1))
                    if h == CK - 1:
                        last.then_inc(projected, 1)

            def project_next(it, j, col, loads):
                if j == 0:
                    pe.wait_ge(w_loaded, loads * 16)
                if j < 2:
                    pe.wait_ge(v_stored, it * 2 + j + 1)
                else:
                    pe.wait_ge(copied, ((it + 1) * NCV + j - 1) * 2)
                project(j, col)

            def project_z(it, e, h, col):
                if h == 0:
                    pe.wait_ge(copied, ((it + 1) * NCV + e + 3) * 2)
                project(NCV + e, col, [h])

            def prepare(it, par):
                c = cv[par]
                pe.wait_ge(gm_ready, it + 1)
                for g in range(2):
                    nc.tensor.matmul(INV[g][:], tri[:, AFTER, :], group(gm, g).rearrange("p u t -> p (u t)"), start=True, stop=False)
                    nc.tensor.matmul(INV[g][:], eye_b[:], negmask[:], start=False, stop=True).then_inc(e_ready, 1)
                    if g == 0:
                        pe.wait_ge(o_stored, it * CH + 1)
                    pe.wait_ge(convolved, (it * NCV + 2) * 3)
                    for n in (2 * g, 2 * g + 1):
                        last = nc.tensor.matmul(TRX[g][:, (n % 2) * 2 * P:(n % 2 + 1) * 2 * P].rearrange("p (a t) -> p a t", a=2),
                                                c[:, KT, n * P:(n + 1) * P], c[:, KT:QT + 1, n * P:(n + 1) * P], start=True, stop=True)
                    last.then_inc(a_ready, 1)
                for n in range(CH):
                    last = nc.tensor.transpose(LOW[0][:, n * P:(n + 1) * P], c[:, KT, n * P:(n + 1) * P], ident[:])
                last.then_inc(k_turned, 1)
                pe.wait_ge(convolved, (it * NCV + NCV) * 3)
                for g in range(2):
                    pe.wait_ge(z_ready, it * HH + g + 1)
                    for n in (2 * g, 2 * g + 1):
                        for e in range(HH):
                            u = HH * (n % 2) + e
                            last = nc.tensor.transpose(PJ[g][:, u * P:(u + 1) * P], c[:, V0 + e, n * P:(n + 1) * P], ident[:])
                    last.then_inc(v_turned, 1)

            def sum_squares(n):
                for e in range(2):
                    last = nc.tensor.matmul(LOW[1][:, 2 * n + e:2 * n + e + 1], sq[:, e, n * P:(n + 1) * P], ones1[:],
                                            start=True, stop=True)
                if n == CH - 1:
                    last.then_inc(summed, 1)

            def turn_x(g, source, bank):
                for u in range(GU):
                    last = nc.tensor.transpose(bank[:, u * P:(u + 1) * P], source[:, GU * g + u, :], ident[:])
                last.then_inc(xt_ready[g], 1)

            def invert(it, fill):
                for g in range(2):
                    pe.wait_ge(e_stored, it * 2 + g + 1)
                    pe.wait_ge(xt_first[g], it + 1)
                    turn_x(g, XT, INV[g])
                for n, b in enumerate(LEVELS):
                    for g in range(2):
                        pe.wait_ge(x_stored[g], it * (LV + 1) + n + 1)
                        for u in range(GU):
                            last = nc.tensor.matmul(INV[g][:, u * HALF:(u + 1) * HALF], Lt[:, GU * g + u, :],
                                                    blocks(X[:, GU * g + u, :], b, 0), start=True, stop=True)
                        last.then_inc(mx_ready[g], 1)
                    fill(2 * n)
                    for g in range(2):
                        pe.wait_ge(t1_ready[g], it * LV + n + 1)
                        if n:
                            pe.wait_ge(xt_stored[g], it * LV + n)
                        for u in range(GU):
                            last = nc.tensor.matmul(INV[g][:, (GU + u) * HALF:(GU + u + 1) * HALF],
                                                    XT[:, GU * g + u, :], T1[:, g, u, :], start=True, stop=True)
                        last.then_inc(xmx_ready[g], 1)
                    fill(2 * n + 1)
                    for g in range(2):
                        pe.wait_ge(x_stored[g], it * (LV + 1) + n + 2)
                        if n == 0:
                            pe.wait_ge(att_stored, it * 2 + g + 1)
                        turn_x(g, X, TRX[g])

            def run_chunks(it, par, col):
                c = cv[par]
                for n in range(CH):
                    k, q = c[:, KT, n * P:(n + 1) * P], c[:, QT, n * P:(n + 1) * P]
                    if n:
                        pe.wait_ge(s_stored, it * N1 + n)
                        nc.tensor.matmul(KS[:, 0:HH * D], k, S[:].rearrange("p e d -> p (e d)"),
                                         start=True, stop=True).then_inc(ks_ready, 1)
                        if n > 1:
                            pe.wait_ge(qs_stored, it * N1 + n - 1)
                        nc.tensor.matmul(QS[:, 0:HH * D], q, S[:].rearrange("p e d -> p (e d)"),
                                         start=True, stop=True).then_inc(qs_ready, 1)
                        if n == 1:
                            pe.wait_ge(squared, it + 2)
                        sum_squares(n if n == N1 else n - 1)
                        pe.wait_ge(r_stored, it * N1 + n)
                    else:
                        project_z(it, 0, 0, col)
                        for g in range(2):
                            pe.wait_ge(xt_stored[g], it * LV + LV)
                        pe.wait_ge(v_stored, it * 2 + 2)
                    for e in range(HH):
                        last = nc.tensor.matmul(UB[:, e * D:(e + 1) * D], XT[:, HH * n + e, :],
                                                R[:, e, :] if n else vn[:, e, :], start=True, stop=True)
                    last.then_inc(u_ready, 1)
                    if n == 0:
                        pe.wait_ge(y_added, it * 2 + 2)
                    if n < N1:
                        project_z(it, (n + 1) // 2, (n + 1) % 2, col)
                        pe.wait_ge(us_stored, it * N1 + n + 1)
                        nc.tensor.matmul(LOW[0][:, 0:HH * D], ktok[:, n, :], us[:].rearrange("p e d -> p (e d)"),
                                         start=True, stop=True).then_inc(ds_ready, 1)
                    pe.wait_ge(u_stored, it * CH + n + 1)
                    if n:
                        pe.wait_ge(o_stored, it * CH + n + 1)
                    for e in range(HH):
                        last = nc.tensor.matmul(OB[:, e * D:(e + 1) * D], attT[:, HH * n + e, :], uh[:, e, :],
                                                start=True, stop=True)
                    last.then_inc(o_ready, 1)
                    if n == N1 - 1:
                        sum_squares(n)

            def turn_outputs(f):
                pe.wait_ge(o_scaled, f + 1)
                for e in range(HH):
                    for n in range(CH):
                        last = nc.tensor.transpose(LOW[e][:, n * P:(n + 1) * P], O[:, HH * n + e, :], ident[:])
                    last.then_inc(ot_ready, 1)

            def project_outputs(f, slot, k):
                if k == 0:
                    pe.wait_ge(gated_ready, f * HH + HH)
                for n in (2 * k, 2 * k + 1):
                    for e in range(HH):
                        last = nc.tensor.matmul(LOW[k][:, (n % 2) * C:(n % 2 + 1) * C], gated[:, e, n * P:(n + 1) * P],
                                                wout[:, bass.ds(slot * (HH * C) + e * C, C)], start=(e == 0), stop=(e == HH - 1))
                last.then_inc(y_ready, 1)

            pe.wait_ge(inits, INITS)
            pe.wait_ge(w_loaded, 16)
            for j in range(NPJ):
                if j >= 2:
                    pe.wait_ge(copied, (j - 1) * 2)
                project(j, 0)
            pe.wait_ge(squared, 1)
            for n in range(CH):
                sum_squares(n)

            def body(it, par, hk, bp):
                col = bp * (2 * T) + T if par == 0 else bp * (-2 * T) + 2 * T
                loads = next_head(par, hk, bp) + 1
                slot = hk + bp if par == 0 else hk + 1

                def fill(s):
                    if s % 2 == 0 and s // 2 < NCV:
                        project_next(it, s // 2, col, loads)
                    elif s == 1:
                        pe.wait_ge(k_stored, it + 1)
                        pe.wait_ge(norms, it * 4 + 1)
                        turn_outputs(it)
                    elif s in (3, 5):
                        project_outputs(it, slot, (s - 3) // 2)
                prepare(it, par)
                invert(it, fill)
                run_chunks(it, par, col)
            iterations(pe, body)
            turn_outputs(ITERS)
            project_outputs(ITERS, NK, 0)
            project_outputs(ITERS, NK, 1)

        @block.scalar
        def _(act):
            def copy_tile(p, par, j, head):
                act.wait_ge(projected, p * NPJ + j + 1)
                nc.scalar.activation(raw[:, j, TAPS - 1:], PJ[j % 2][:], ACT.Copy).then_inc(copied, 1)
                nc.scalar.activation(cv[par][:, j, :], PJ[j % 2][:], ACT.Copy,
                                     scale=convw[:, bass.ds(head * (NCV * TAPS) + j * TAPS + TAPS - 1, 1)]).then_inc(copied, 1)

            def tanh_tile(p, e):
                act.wait_ge(projected, p * NPJ + NCV + e + 1)
                nc.scalar.activation(zt[:, e, :], PJ[e][:], ACT.Tanh, scale=0.5).then_inc(tanh_done, 1)

            def squares(n):
                for u in range(HH * n, HH * (n + 1)):
                    last = nc.scalar.activation(junk[:, u, :], O[:, u, :], ACT.Square, accum_out=ssq[:, u:u + 1])
                if n == CH - 1:
                    last.then_inc(ssq_ready, 1)

            act.wait_ge(inits, INITS)
            for j in range(NCV):
                copy_tile(0, 0, j, 0)
            for e in range(HH):
                tanh_tile(0, e)
            for n in range(CH):
                squares(n)

            def body(it, par, hk, bp):
                for g in range(2):
                    act.wait_ge(e_ready, it * 2 + g + 1)
                    nc.scalar.activation(group(E, g)[:, :, 1:], units(INV[g][:]), ACT.Exp).then_inc(e_stored, 1)
                act.wait_ge(k_turned, it + 1)
                nc.scalar.activation(ktok[:].rearrange("p n d -> p (n d)"), LOW[0][:], ACT.Copy).then_inc(k_stored, 1)
                for g in range(2):
                    act.wait_ge(xt_ready[g], it * (LV + 1) + 1)
                    nc.scalar.activation(group(X, g), units(INV[g][:]), ACT.Copy).then_inc(x_stored[g], 1)
                for n, b in enumerate(LEVELS):
                    if n < NCV:
                        act.wait_ge(convolved, (it * NCV + n + 1) * 3)
                        copy_tile(it + 1, 1 - par, n, next_head(par, hk, bp))
                    for g in range(2):
                        act.wait_ge(xt_ready[g], it * (LV + 1) + n + 2)
                        nc.scalar.activation(blocks(group(XT, g), b, 1), blocks(units(TRX[g][:]), b, 1),
                                             ACT.Copy).then_inc(xt_stored[g], 1)
                for n in range(CH):
                    if n:
                        act.wait_ge(qs_ready, it * N1 + n)
                        if n > 1:
                            act.wait_ge(o_stored, it * CH + n + 1)
                        for e in range(HH):
                            last = nc.scalar.activation(qss[:, e, :], QS[:, e * D:(e + 1) * D], ACT.Copy,
                                                        scale=gt[par][:, G_INCL, HH * n + e:HH * n + e + 1])
                        last.then_inc(qs_stored, 1)
                    act.wait_ge(u_ready, it * CH + n + 1)
                    if n < N1:
                        act.wait_ge(us_stored, it * N1 + n + 1)
                    nc.scalar.activation(uh[:].rearrange("p e d -> p (e d)"), UB[:, 0:HH * D], ACT.Copy).then_inc(u_stored, 1)
                    if n:
                        if n <= HH:
                            tanh_tile(it + 1, n - 1)
                        act.wait_ge(o_stored, it * CH + n + 1)
                        squares(n - 1)
                act.wait_ge(o_stored, it * CH + CH + 1)
                squares(CH - 1)
            iterations(act, body)

        @block.gpsimd
        def _(pool):
            def fetch_gates(it, par):
                nc.gpsimd.tensor_copy(gt[par][:].rearrange("p q u -> p (q u)"), gates[:, bass.ds(it * (NG * U), NG * U)]).then_inc(gates_here, 1)
                pool.wait_ge(gates_here, it + 1)
                nc.gpsimd.tensor_tensor(gm[:], tri[:, UPTO, :].unsqueeze(1).broadcast_to((P, U, P)),
                                        gt[par][:, G_LOG, :].unsqueeze(2).broadcast_to((P, U, P)), ALU.mult).then_inc(gm_ready, 1)

            def squares(p, par):
                pool.wait_ge(convolved, (p * NCV + 2) * 3)
                nc.gpsimd.tensor_tensor(sq[:], cv[par][:, 0:2, :], cv[par][:, 0:2, :], ALU.mult).then_inc(squared, 1)

            def scale_outputs(f):
                pool.wait_ge(ms_step, f * 2 + 2)
                nc.gpsimd.tensor_tensor(rms[:], ms[:], halves[:, 1, :], ALU.pow).then_inc(pool_step, 1)
                pool.wait_ge(pool_step, f + 1)
                nc.gpsimd.tensor_tensor(O[:], O[:], rms[:].unsqueeze(2).broadcast_to((P, U, D)), ALU.mult).then_inc(o_scaled, 1)

            def first_xt():
                even = columns(ident[:], 0).unsqueeze(1).broadcast_to((P, U, HALF))
                nc.gpsimd.tensor_tensor(columns(XT[:], 0), even, even, ALU.mult).then_inc(xt_init, 1)

            def root_norms(p, par):
                pool.wait_ge(norms, p * 4 + 1)
                nc.gpsimd.tensor_tensor(nk[:], n2[par][:, :, 0], halves[:, 0, 0:CH], ALU.pow).then_inc(nk_ready, 1)

            nc.gpsimd.memset(halves[:, 0, :], 0.5).then_inc(inits, 1)
            nc.gpsimd.memset(halves[:, 1, :], -0.5).then_inc(inits, 1)
            pool.wait_ge(inits, INITS)
            fetch_gates(0, 0)
            squares(0, 0)
            first_xt()
            root_norms(0, 0)

            def body(it, par, hk, bp):
                scale_outputs(it)
                pool.wait_ge(e_ready, it * 2 + 2)
                fetch_gates(it + 1, 1 - par)
                pool.wait_ge(summed, it + 1)
                squares(it + 1, 1 - par)
                pool.wait_ge(u_ready, it * CH + CH)
                first_xt()
                root_norms(it + 1, 1 - par)
            iterations(pool, body)
            scale_outputs(ITERS)

        @block.vector
        def _(dve):
            def tap(p, par, step, head):
                j, k = step // 3, TAPS - 2 - step % 3
                if step % 3 == 0:
                    dve.wait_ge(copied, (p * NCV + j + 1) * 2)
                else:
                    dve.wait_ge(convolved, p * (NCV * 3) + step)
                nc.vector.scalar_tensor_tensor(cv[par][:, j, :], raw[:, j, k:k + T], convw[:, bass.ds(head * (NCV * TAPS) + j * TAPS + k, 1)],
                                               cv[par][:, j, :], ALU.mult, ALU.add).then_inc(convolved, 1)

            def gate_z(p, par, e):
                dve.wait_ge(tanh_done, p * HH + e + 1)
                nc.vector.scalar_tensor_tensor(zs[par][:, e, :], zt[:, e, :], 1.0, PJ[e][:], ALU.add, ALU.mult).then_inc(z_ready, 1)

            def prepare_norms(p, par):
                dve.wait_ge(summed, p + 1)
                nc.vector.tensor_scalar(n2[par][:].rearrange("p n e -> p (n e)"), LOW[1][:, 0:2 * CH], NORM_EPS ** 2, None, ALU.max).then_inc(norms, 1)
                dve.wait_ge(norms, p * 4 + 1)
                nc.vector.reciprocal(rk2[:], n2[par][:, :, 0]).then_inc(norms, 1)
                dve.wait_ge(norms, p * 4 + 2)
                dve.wait_ge(gates_here, p + 1)
                nc.vector.tensor_tensor(cs[:].rearrange("p (n e) -> p n e", e=HH), gt[par][:, G_BETA, :].rearrange("p (n e) -> p n e", e=HH),
                                        rk2[:].unsqueeze(2).broadcast_to((P, CH, HH)), ALU.mult).then_inc(norms, 1)
                dve.wait_ge(norms, p * 4 + 3)
                nc.vector.tensor_tensor(cr[:], cs[:], gt[par][:, G_REST, :], ALU.mult).then_inc(norms, 1)

            def mean_squares(f, par):
                nc.vector.tensor_scalar(eq[:], n2[par][:, :, 1], RMS_EPS, None, ALU.mult).then_inc(ms_step, 1)
                dve.wait_ge(ms_step, f * 2 + 1)
                dve.wait_ge(ssq_ready, f + 1)
                nc.vector.scalar_tensor_tensor(ms[:].rearrange("p (n e) -> p n e", e=HH), ssq[:].rearrange("p (n e) -> p n e", e=HH), 1.0 / D,
                                               eq[:].unsqueeze(2).broadcast_to((P, CH, HH)), ALU.mult, ALU.add).then_inc(ms_step, 1)

            def gate_outputs(f, par):
                for e in range(HH):
                    dve.wait_ge(ot_ready, f * HH + e + 1)
                    nc.vector.tensor_tensor(gated[:, e, :], LOW[e][:], zs[par][:, e, :], ALU.mult).then_inc(gated_ready, 1)

            def add_y(f, tile, k):
                dve.wait_ge(y_ready, f * 2 + k + 1)
                part = x[:, bass.ds(tile * C + 2 * k * C, 2 * C)]
                nc.vector.tensor_tensor(part, part, LOW[k][:], ALU.add).then_inc(y_added, 1)

            nc.vector.memset(raw[:, :, 0:TAPS - 1], 0.0).then_inc(inits, 1)
            nc.vector.memset(E[:, :, 0:1], 0.0).then_inc(inits, 1)
            nc.vector.memset(n2[1][:], 1.0).then_inc(inits, 1)
            nc.vector.memset(zs[1][:], 0.0).then_inc(inits, 1)
            nc.vector.memset(O[:], 0.0).then_inc(inits, 1)
            dve.wait_ge(inits, INITS)
            nc.vector.nop().then_inc(o_stored, 1)
            for step in range(3 * NCV):
                tap(0, 0, step, 0)
            for e in range(HH):
                gate_z(0, 0, e)
            prepare_norms(0, 0)

            def body(it, par, hk, bp):
                g_ = gt[par]
                mean_squares(it, 1 - par)

                def products(dst, g, part, decays, done):
                    for u in range(GU * g, GU * (g + 1)):
                        at = (u // HH % 2) * 2 * P + part * P
                        last = nc.vector.scalar_tensor_tensor(dst[:, u, :], TRX[g][:, at:at + P], cs[:, u:u + 1], E[:, u, decays:decays + P],
                                                              ALU.mult, ALU.mult)
                    last.then_inc(done, 1)

                def store_v(g):
                    dve.wait_ge(v_turned, it * 2 + g + 1)
                    for n in (2 * g, 2 * g + 1):
                        at = (n % 2) * HH * D
                        last = nc.vector.tensor_scalar(vn[:, HH * n:HH * (n + 1), :].rearrange("p e d -> p (e d)"), PJ[g][:, at:at + HH * D],
                                                       nk[:, n:n + 1], None, ALU.mult)
                    last.then_inc(v_stored, 1)
                dve.wait_ge(norms, it * 4 + 3)
                for g in range(2):
                    dve.wait_ge(a_ready, it * 2 + g + 1)
                    dve.wait_ge(e_stored, it * 2 + g + 1)
                    products(Lt, g, 0, 0, lt_stored)
                    if g == 0:
                        dve.wait_ge(xt_init, it + 1)
                    dve.wait_ge(lt_stored, it * 2 + g + 1)
                    nc.vector.scalar_tensor_tensor(columns(group(XT, g), 1), columns(group(Lt, g), 1), odd[:, 0:1],
                                                   first[:].unsqueeze(1).broadcast_to((P, GU, HALF)),
                                                   ALU.subtract, ALU.mult).then_inc(xt_first[g], 1)
                dve.wait_ge(nk_ready, it + 1)
                store_v(0)
                head, p = next_head(par, hk, bp), it + 1
                tile = bp * (-2 * CH) + 3 * CH if par == 0 else bp * (2 * CH)

                def fill(s):
                    if s == 2:
                        gate_outputs(it, 1 - par)
                    if s in (5, 6):
                        add_y(it, tile, s - 5)
                    if s >= 2:
                        tap(p, 1 - par, s - 2, head)
                for n, b in enumerate(LEVELS):
                    for g in range(2):
                        dve.wait_ge(mx_ready[g], it * LV + n + 1)
                        nc.vector.tensor_tensor(T1[:, g], INV[g][:, 0:GU * HALF].rearrange("p (u t) -> p u t", u=GU),
                                                lmask[:, n, :].unsqueeze(1).broadcast_to((P, GU, HALF)), ALU.mult).then_inc(t1_ready[g], 1)
                        if n == 0:
                            products(attT, g, 1, 1, att_stored)
                    if n == 0:
                        store_v(1)
                    fill(2 * n)
                    for g in range(2):
                        dve.wait_ge(xmx_ready[g], it * LV + n + 1)
                        xe = blocks(group(X, g), b, 0)
                        nc.vector.tensor_tensor(xe, xe, INV[g][:, GU * HALF:].rearrange("p (u n b) -> p u n b", u=GU, b=b),
                                                ALU.subtract).then_inc(x_stored[g], 1)
                    fill(2 * n + 1)
                for n in range(CH):
                    if n:
                        dve.wait_ge(ks_ready, it * N1 + n)
                        for e in range(HH):
                            u = HH * n + e
                            last = nc.vector.scalar_tensor_tensor(R[:, e, :], KS[:, e * D:(e + 1) * D], g_[:, G_NPREV, u:u + 1],
                                                                  vn[:, u, :], ALU.mult, ALU.add)
                        last.then_inc(r_stored, 1)
                    if n < N1:
                        dve.wait_ge(u_ready, it * CH + n + 1)
                        for e in range(HH):
                            u = HH * n + e
                            last = nc.vector.tensor_scalar(us[:, e, :], UB[:, e * D:(e + 1) * D], cr[:, u:u + 1], None, ALU.mult)
                        last.then_inc(us_stored, 1)
                        dve.wait_ge(ds_ready, it * N1 + n + 1)
                        if n == 0:
                            last = nc.vector.tensor_copy(S[:].rearrange("p e d -> p (e d)"), LOW[0][:, 0:HH * D])
                        else:
                            for e in range(HH):
                                u = HH * n + e
                                last = nc.vector.scalar_tensor_tensor(S[:, e, :], S[:, e, :], g_[:, G_TOTAL, u:u + 1],
                                                                      LOW[0][:, e * D:(e + 1) * D], ALU.mult, ALU.add)
                        last.then_inc(s_stored, 1)
                    if n == N1:
                        prepare_norms(p, 1 - par)
                        gate_z(p, 1 - par, 1)
                    dve.wait_ge(o_ready, it * CH + n + 1)
                    o = O[:, HH * n:HH * (n + 1), :].rearrange("p e d -> p (e d)")
                    if n == 0:
                        nc.vector.tensor_copy(o, OB[:, 0:HH * D]).then_inc(o_stored, 1)
                    else:
                        dve.wait_ge(qs_stored, it * N1 + n)
                        nc.vector.tensor_tensor(o, OB[:, 0:HH * D], qss[:].rearrange("p e d -> p (e d)"), ALU.add).then_inc(o_stored, 1)
                    if n < 2:
                        tap(p, 1 - par, 3 * NCV - 2 + n, head)
                    elif n == 2:
                        gate_z(p, 1 - par, 0)
            iterations(dve, body)
            mean_squares(ITERS, (ITERS - 1) % 2)
            gate_outputs(ITERS, (ITERS - 1) % 2)
            for k in range(2):
                add_y(ITERS, CH * (B - 1), k)



SPL_OUT, SPL_COMPRESSION = 1024, 128.9
SPL_N = SPL_OUT * C
SPL_CTRL = max(16, int(SPL_N / SPL_COMPRESSION))
SPL_ROWS = SPL_N // P
SPL_TILES = SPL_ROWS // P
SPL_TAPS = 5
FF1 = SPL_OUT // P
DIM2 = 704
FF2 = -(-DIM2 // P)
ZERO_POINT = 128.0


def spline_constants():
    t = np.linspace(0.0, SPL_CTRL - 1.0, SPL_N, dtype=np.float64)
    i = np.clip(np.floor(t).astype(np.int64), 0, SPL_CTRL - 2)
    f = (t - i).astype(np.float32).astype(np.float64)
    basis = 0.5 * np.stack([-f + 2 * f ** 2 - f ** 3, 2 - 5 * f ** 2 + 3 * f ** 3, f + 4 * f ** 2 - 3 * f ** 3, -f ** 2 + f ** 3])
    first = i[::P]
    step = i - np.repeat(first, P)
    assert step.max() == 1
    weights = np.zeros((SPL_TAPS, SPL_N))
    for k in range(4):
        weights[k + step, np.arange(SPL_N)] = basis[k]
    points = np.clip(first[None, :] - 1 + np.arange(SPL_TAPS)[:, None], 0, SPL_CTRL - 1)
    return points, weights.astype(np.float32)


def spline_weights(nc, sem, banks, keep, ins):
    ident = keep["ident"]
    with ExitStack() as ctx:
        def sb(n, shape, dt=FP32):
            return ctx.enter_context(nc.sbuf_tensor("spl_" + n, shape, dt))
        basis = sb("basis", [P, 2, SPL_TAPS, P])
        points = sb("points", [P, SPL_TILES, 3, SPL_TAPS])
        rows = sb("rows", [P, 2, 3, P])
        loaded, basis_loaded = sem("spl_points_loaded"), [sem(f"spl_basis_loaded{i}") for i in range(2)]
        step, ready, turned, stored = sem("spl_step"), sem("spl_ready"), sem("spl_turned"), sem("spl_stored")
        block = ctx.enter_context(nc.Block())

        @block.sync
        def _(sp):
            sp.dma_start(points[:], ins["spl_points"]).then_inc(loaded, 16)
            for a in range(SPL_TILES):
                if a >= 2:
                    sp.wait_ge(ready, a - 1)
                sp.dma_start(basis[:, a % 2], ins["spl_basis"][a]).then_inc(basis_loaded[a % 2], 16)

        @block.vector
        def _(dve):
            dve.wait_ge(loaded, 16)
            for a in range(SPL_TILES):
                dve.wait_ge(basis_loaded[a % 2], 16 * (a // 2 + 1))
                if a >= 2:
                    dve.wait_ge(turned, a - 1)
                for k in range(SPL_TAPS):
                    for m in range(3):
                        dst, scalar = rows[:, a % 2, m, :], points[:, a, m, k:k + 1]
                        if k == 0:
                            nc.vector.tensor_scalar(dst, basis[:, a % 2, k, :], scalar, None, ALU.mult).then_inc(step, 1)
                        else:
                            dve.wait_ge(step, (a * SPL_TAPS + k - 1) * 3 + m + 1)
                            nc.vector.scalar_tensor_tensor(dst, basis[:, a % 2, k, :], scalar, dst, ALU.mult, ALU.add).then_inc(step, 1)
                dve.wait_ge(step, (a + 1) * SPL_TAPS * 3)
                nc.vector.nop().then_inc(ready, 1)

        @block.tensor
        def _(pe):
            for a in range(SPL_TILES):
                pe.wait_ge(ready, a + 1)
                if a >= 2:
                    pe.wait_ge(stored, 3 * (a - 1))
                for m in range(3):
                    last = nc.tensor.transpose(banks[a % 2][:, m * P:(m + 1) * P], rows[:, a % 2, m, :], ident[:])
                last.then_inc(turned, 1)

        @block.scalar
        def _(act):
            per = P // CK
            for a in range(SPL_TILES):
                act.wait_ge(turned, a + 1)
                for m, dst in enumerate((keep["wg1"], keep["wu1"])):
                    nc.scalar.activation(dst[:].rearrange("p h i -> p i h")[:, a * per:(a + 1) * per, :],
                                         banks[a % 2][:, m * P:(m + 1) * P].rearrange("p (i h) -> p i h", h=CK), ACT.Copy).then_inc(stored, 1)
                cols = P // FF1
                nc.scalar.activation(keep["wd1"][:].rearrange("p i c -> p c i")[:, a * cols:(a + 1) * cols, :],
                                     banks[a % 2][:, 2 * P:3 * P].rearrange("p (c i) -> p c i", i=FF1), ACT.Copy).then_inc(stored, 1)


def norm_phase(nc, sem, banks, keep, name):
    with ExitStack() as ctx:
        v, g, t, s, _ = layer_norm(nc, ctx, sem, name, keep["x"], keep["xnT"], keep["ident"], banks[0:4])
        block = ctx.enter_context(nc.Block())
        block.vector(lambda dve: v(dve))
        block.gpsimd(g)
        block.tensor(t)
        block.scalar(s)


def ffn(nc, sem, banks, keep, name, wg, wu, wd, inner, sg_scale=None, su_scale=None):
    x, xnT = keep["x"], keep["xnT"]
    tiles = inner // P
    with ExitStack() as ctx:
        sg = ctx.enter_context(nc.sbuf_tensor(name + "_sg", [P, 2, T], FP32))
        hid = ctx.enter_context(nc.sbuf_tensor(name + "_hid", [P, 2, T], FP32))
        GATE, UP, Y = banks[0:2], banks[2:4], banks[4:8]
        gate_ready, up_ready, silu_done, hid_ready = (sem(f"{name}_{n}") for n in ("gate", "up", "silu", "hid"))
        down_done, y_ready, y_added = (sem(f"{name}_{n}") for n in ("down", "y", "y_added"))
        block = ctx.enter_context(nc.Block())
        NB = B

        @block.tensor
        def _(pe):
            def gate_up(blk, i, first):
                if not (first and i < 2):
                    pe.wait_ge(silu_done, blk * tiles + i - 1)
                for h in range(CK):
                    last = nc.tensor.matmul(GATE[i % 2][:, :], wg[:, h, i * P:(i + 1) * P], xnT[:, h, bass.ds(blk * T, T)],
                                            start=(h == 0), stop=(h == CK - 1))
                last.then_inc(gate_ready, 1)
                if not (first and i < 2):
                    pe.wait_ge(hid_ready, blk * tiles + i - 1)
                for h in range(CK):
                    last = nc.tensor.matmul(UP[i % 2][:, :], wu[:, h, i * P:(i + 1) * P], xnT[:, h, bass.ds(blk * T, T)],
                                            start=(h == 0), stop=(h == CK - 1))
                last.then_inc(up_ready, 1)

            def down(blk, i, first):
                pe.wait_ge(hid_ready, blk * tiles + i + 1)
                if i == 0 and not first:
                    pe.wait_ge(y_added, blk * CH)
                for n in range(CH):
                    last = nc.tensor.matmul(Y[n][:, 0:C], hid[:, i % 2, n * P:(n + 1) * P], wd[:, i, :],
                                            start=(i == 0), stop=(i == tiles - 1))
                    if i == tiles - 1:
                        last.then_inc(y_ready, 1)
                if i < tiles - 1:
                    last.then_inc(down_done, 1)

            def body(blk, first):
                for i in range(tiles):
                    gate_up(blk, i, first)
                    if i:
                        down(blk, i - 1, first)
                down(blk, tiles - 1, first)
            assert tiles % 2 == 0
            body(0, True)
            with pe.Fori(1, NB) as blk:
                body(blk, False)

        @block.scalar
        def _(act):
            def body(blk, first):
                for i in range(tiles):
                    act.wait_ge(gate_ready, blk * tiles + i + 1)
                    if not (first and i < 2):
                        act.wait_ge(hid_ready, blk * tiles + i - 1)
                    nc.scalar.activation(sg[:, i % 2, :], GATE[i % 2][:, :], ACT.Silu,
                                         scale=1.0 if sg_scale is None else sg_scale[:, i:i + 1]).then_inc(silu_done, 1)
            body(0, True)
            with act.Fori(1, NB) as blk:
                body(blk, False)

        @block.vector
        def _(dve):
            def body(blk, first):
                for i in range(tiles):
                    dve.wait_ge(silu_done, blk * tiles + i + 1)
                    dve.wait_ge(up_ready, blk * tiles + i + 1)
                    if i >= 2:
                        dve.wait_ge(down_done, blk * (tiles - 1) + i - 1)
                    if su_scale is None:
                        last = nc.vector.tensor_tensor(hid[:, i % 2, :], UP[i % 2][:, :], sg[:, i % 2, :], ALU.mult)
                    else:
                        last = nc.vector.scalar_tensor_tensor(hid[:, i % 2, :], UP[i % 2][:, :], su_scale[:, i:i + 1],
                                                              sg[:, i % 2, :], ALU.mult, ALU.mult)
                    last.then_inc(hid_ready, 1)
                for n in range(CH):
                    dve.wait_ge(y_ready, blk * CH + n + 1)
                    part = x[:, bass.ds(blk * (CH * C) + n * C, C)]
                    nc.vector.tensor_tensor(part, part, Y[n][:, 0:C], ALU.add).then_inc(y_added, 1)
            body(0, True)
            with dve.Fori(1, NB) as blk:
                body(blk, False)



KVH, GRP, HD = 8, 4, 8
TH = P // (GRP * HD)
HEADS = TH * GRP
ROPE_BASE = 10000.0
STEP_HEADS = [max(1, T // P // (i + 1)) for i in range(CH)]
STEPS = [(i, s) for i in range(CH) for s in range(HEADS // STEP_HEADS[i])]
SCALE = float(1.0 / np.sqrt(HD))


def attention(nc, sem, banks, keep, ins):
    x, xnT, ident, eye_b = (keep[k] for k in ("x", "xnT", "ident", "eye_b"))
    NS1 = len(STEPS)
    NS = 2 * NS1
    L1, L2 = 3, 4
    VW = TH * HD
    with ExitStack() as ctx:
        def sb(n, shape, dt=FP32):
            return ctx.enter_context(nc.sbuf_tensor("at_" + n, shape, dt))
        w = sb("w", [P, 2, 4, CK, P])
        wv = sb("wv", [P, CK, KVH * HD])
        wo = sb("wo", [P, 2 * C])
        bias = sb("bias", [P, 2, 4])
        bv = sb("bv", [P, KVH * HD])
        bo = sb("bo", [P, C])
        cosines, sines = sb("cosines", [P, T]), sb("sines", [P, T])
        gmask = sb("gmask", [P, GRP])
        own = sb("own", [P, TH])
        cmask = keep["cmask"]
        ta, tb = sb("ta", [P, 2, T]), sb("tb", [P, 2, T])
        qk = [sb(f"qk{i}", [P, 2, T]) for i in range(2)]
        kp = [sb(f"kp{i}", [P, GRP, T]) for i in range(2)]
        v = [sb(f"v{i}", [P, CH, VW]) for i in range(2)]
        mx, nmx = sb("mx", [P, 4, GRP]), sb("nmx", [P, 4, GRP])
        prob = sb("prob", [P, 4, T])
        probT = sb("probT", [P, 3, T])
        rsum, rinv = sb("rsum", [P, 4, GRP]), sb("rinv", [P, 2, GRP])
        yT = sb("yT", [P, P])
        xs = sb("xs", [P, CK, T])
        SC, PT, YB, FB = banks[0:3], banks[3:5], banks[5:7], banks[7]
        loaded, bo_added = sem("at_loaded"), sem("at_bo_added")
        xs_ready = sem("at_xs")
        qk_ready, v_ready = sem("at_qk"), sem("at_v")
        rope, qk_done, kp_done, v_done = sem("at_rope"), sem("at_qk_done"), sem("at_kp"), sem("at_v_done")
        s_ready, mx_step, p_ready, pt_ready = sem("at_s"), sem("at_mx"), sem("at_p"), sem("at_pt")
        rinv_ready, pn_ready = sem("at_rinv"), sem("at_pn")
        pt_stored, pv_done = sem("at_pt_stored"), sem("at_pv")
        yt_step, out_ready, fb_read = (sem("at_" + n) for n in ("yt_step", "out", "fb_read"))
        loads = [(w[:, 0], ins["at_w"][0]), (w[:, 1], ins["at_w"][1]), (wv[:], ins["at_wv"]), (wo[:], ins["at_wo"]),
                 (bias[:], ins["at_bias"]), (bv[:], ins["at_bv"].partition_broadcast(P)),
                 (bo[:], ins["at_bo"].partition_broadcast(P)), (cosines[:], ins["cosines"]), (sines[:], ins["sines"]),
                 (gmask[:], ins["gmask"]), (own[:], ins["own"])]
        ALL_LOADED = 16 * len(loads)
        fetch_quantised, convert_quantised = dequantise(nc, ctx, sem, keep, ins)
        block = ctx.enter_context(nc.Block())

        def iterations(eng, body):
            with eng.Fori(0, B - 1) as b:
                body(b, False)
            body(B - 1, True)

        def place(s):
            i, k = STEPS[s % NS1]
            return s // NS1, i, k, HEADS // STEP_HEADS[i]

        def heads(s):
            t_, i, k, m = place(s)
            g = STEP_HEADS[i]
            return [(n, (k * g + n) // GRP, (k * g + n) % GRP) for n in range(g)], (i + 1) * P, i

        def prefetch(s):
            t_, i, k, m = place(s)
            return (k - 4) // 2 if i == 2 and k >= 4 and k % 2 == 0 and k <= 12 else None

        def fb_uses(b, t_, i=None, n=None):
            before = b * 18 + 5 + t_ * 9
            if n is not None:
                return before + 2 + n
            skipped = 5 if t_ == 1 and isinstance(b, int) and b == B - 1 else 0
            return before + (i if i < 2 else i + 5 - skipped)

        @block.sync
        def _(sp):
            for dst, src in loads:
                sp.dma_start(dst, src).then_inc(loaded, 16)
            fetch_quantised(sp)

        @block.tensor
        def _(pe):
            def project(item, t_, n):
                if n < 4:
                    for h in range(CK):
                        last = nc.tensor.matmul(FB[:], w[:, t_, n, h, :], xs[:, h, :], start=(h == 0), stop=(h == CK - 1))
                    last.then_inc(qk_ready, 1)
                else:
                    for c in range(CH):
                        for h in range(CK):
                            last = nc.tensor.matmul(FB[:, c * VW:(c + 1) * VW], xs[:, h, c * P:(c + 1) * P],
                                                    wv[:, h, t_ * VW:(t_ + 1) * VW], start=(h == 0), stop=(h == CK - 1))
                    last.then_inc(v_ready, 1)

            def scores(b, s):
                hs, n, i = heads(s)
                t_ = s // NS1
                if s % NS1 == 0:
                    pe.wait_ge(kp_done, b * 2 + t_ + 1)
                if s >= 3:
                    pe.wait_ge(p_ready, b * NS + s - 2)
                if i == 0:
                    nc.tensor.matmul(SC[s % 3][:, 0:len(hs) * P].rearrange("p (k n) -> p k n", n=P), eye_b[:],
                                     cmask[:].unsqueeze(1).broadcast_to((P, len(hs), P)), start=True, stop=False)
                for k, th, g in hs:
                    rows = slice(GRP * HD * th, GRP * HD * (th + 1))
                    last = nc.tensor.matmul(SC[s % 3][:, k * n:(k + 1) * n], qk[t_][rows, 0, i * P:(i + 1) * P], kp[t_][rows, g, 0:n],
                                            start=(i > 0), stop=(i == 0 and k == len(hs) - 1))
                    if i:
                        last = nc.tensor.matmul(SC[s % 3][:, (k + 1) * n - P:(k + 1) * n], eye_b[:], cmask[:], start=False, stop=True)
                last.then_inc(s_ready, 1)

            def turn(b, s):
                hs, n, i = heads(s)
                pe.wait_ge(pn_ready, b * NS + s + 1)
                if s >= 2:
                    pe.wait_ge(pt_stored, b * NS + s - 1)
                for k in range(len(hs) * (i + 1)):
                    last = nc.tensor.transpose(PT[s % 2][:, k * P:(k + 1) * P], prob[:, s % 4, k * P:(k + 1) * P], ident[:])
                last.then_inc(pt_ready, 1)

            def times_v(b, s):
                hs, n, i = heads(s)
                t_, _, k_, m = place(s)
                pe.wait_ge(pt_stored, b * NS + s + 1)
                if s % NS1 == 0:
                    pe.wait_ge(v_done, b * 2 + t_ + 1)
                if k_ == 0 and t_ * CH + i >= 2:
                    pe.wait_ge(yt_step, (b * 8 + t_ * CH + i - 1) * TH)
                for k, th, g in hs:
                    for c in range(i + 1):
                        last = nc.tensor.matmul(YB[i % 2][VW * g:VW * (g + 1), th * P:(th + 1) * P], v[t_][:, c, :],
                                                probT[:, s % 3, k * n + c * P:k * n + (c + 1) * P], start=(c == 0), stop=(c == i))
                last.then_inc(pv_done, 1)

            def project_y(b, t_, i):
                pe.wait_ge(yt_step, (b * 8 + t_ * CH + i + 1) * TH)
                pe.wait_ge(fb_read, fb_uses(b, t_, i))
                nc.tensor.matmul(FB[:, 0:C], yT[:], wo[:, t_ * C:(t_ + 1) * C], start=True, stop=True).then_inc(out_ready, 1)

            pe.wait_ge(loaded, ALL_LOADED)
            pe.wait_ge(xs_ready, 1)
            for n in range(5):
                if n:
                    pe.wait_ge(fb_read, n)
                project(0, 0, n)

            def body(b, final):
                for s in range(NS + L2):
                    if s < NS:
                        scores(b, s)
                    if L1 <= s < NS + L1:
                        turn(b, s - L1)
                    if s >= L2:
                        times_v(b, s - L2)
                        t_, i, k, m = place(s - L2)
                        before = (t_, i - 1) if i else (t_ - 1, CH - 1)
                        if before[0] >= 0 and k == 2:
                            project_y(b, *before)
                        n = prefetch(s - L2)
                        if n is not None and not (final and t_ == 1):
                            if n == 0 and t_ == 1:
                                pe.wait_ge(xs_ready, b + 2)
                            pe.wait_ge(fb_read, fb_uses(b, t_, n=n))
                            project(b * 2 + t_ + 1, 1 - t_, n)
                project_y(b, 1, CH - 1)
                pe.wait_ge(fb_read, fb_uses(b, 1, CH - 1) + 1)
            iterations(pe, body)

        @block.scalar
        def _(act):
            act.wait_ge(loaded, ALL_LOADED)

            def fetch_xs(b):
                nc.scalar.activation(xs[:], xnT[:, :, bass.ds(b * T, T)], ACT.Copy).then_inc(xs_ready, 1)

            def store(b, s):
                hs, n, i = heads(s)
                act.wait_ge(pt_ready, b * NS + s + 1)
                if s >= 3:
                    act.wait_ge(pv_done, b * NS + s - 2)
                nc.scalar.activation(probT[:, s % 3, 0:len(hs) * n], PT[s % 2][:, 0:len(hs) * n], ACT.Copy).then_inc(pt_stored, 1)

            fetch_xs(0)

            def body(b, final):
                for s in range(NS + L1):
                    if s >= L1:
                        store(b, s - L1)
                    if s < NS:
                        hs, n, i = heads(s)
                        act.wait_ge(mx_step, (b * NS + s + 1) * 2)
                        if s >= 4:
                            act.wait_ge(pt_ready, b * NS + s - 3)
                        for k, th, g in hs:
                            last = nc.scalar.activation(prob[:, s % 4, k * n:(k + 1) * n], SC[s % 3][:, k * n:(k + 1) * n], ACT.Exp,
                                                        bias=nmx[:, s % 4, k:k + 1], scale=SCALE, accum_out=rsum[:, s % 4, k:k + 1])
                        last.then_inc(p_ready, 1)
                    if s == NS1 + L2 + 2 and not final:
                        act.wait_ge(v_ready, b * 2 + 2)
                        fetch_xs(b + 1)
            iterations(act, body)

        @block.gpsimd
        def _(pool):
            def rotate(item, t_):
                for n in range(2):
                    pool.wait_ge(rope, item * 4 + 2 * n + 2)
                    nc.gpsimd.tensor_tensor(qk[t_][:, n, :], ta[:, n, :], tb[:, n, :], ALU.add).then_inc(qk_done, 1)
                pool.wait_ge(qk_done, item * 2 + 2)
                nc.gpsimd.tensor_tensor(kp[t_][:], qk[t_][:, 1, :].unsqueeze(1).broadcast_to((P, GRP, T)),
                                        gmask[:].unsqueeze(2).broadcast_to((P, GRP, T)), ALU.mult).then_inc(kp_done, 1)
            pool.wait_ge(loaded, ALL_LOADED)
            rotate(0, 0)
            xv = x[:].rearrange("p (t c) -> p t c", c=C)
            nc.gpsimd.tensor_tensor(xv, xv, bo[:].unsqueeze(1).broadcast_to((P, TILES, C)), ALU.add).then_inc(bo_added, 1)
            convert_quantised(pool)
            with pool.Fori(0, B - 1) as b:
                rotate(b * 2 + 1, 1)
                rotate(b * 2 + 2, 0)
            rotate(B * 2 - 1, 1)

        @block.vector
        def _(dve):
            def take(item, t_, n):
                if n < 4:
                    dve.wait_ge(qk_ready, item * 4 + n + 1)
                    nc.vector.scalar_tensor_tensor((ta if n % 2 == 0 else tb)[:, n // 2, :], FB[:], bias[:, t_, n:n + 1],
                                                   (cosines if n % 2 == 0 else sines)[:], ALU.add, ALU.mult).then_inc(rope, 1)
                    dve.wait_ge(rope, item * 4 + n + 1)
                    nc.vector.nop().then_inc(fb_read, 1)
                else:
                    dve.wait_ge(v_ready, item + 1)
                    nc.vector.tensor_tensor(v[t_][:], FB[:, 0:CH * VW].rearrange("p (n d) -> p n d", n=CH),
                                            bv[:, t_ * VW:(t_ + 1) * VW].unsqueeze(1).broadcast_to((P, CH, VW)),
                                            ALU.add).then_inc(v_done, 1)
                    dve.wait_ge(v_done, item + 1)
                    nc.vector.nop().then_inc(fb_read, 1)

            def normalise(b, s):
                hs, n, i = heads(s)
                g = len(hs)
                dve.wait_ge(p_ready, b * NS + s + 1)
                nc.vector.reciprocal(rinv[:, s % 2, 0:g], rsum[:, s % 4, 0:g]).then_inc(rinv_ready, 1)
                dve.wait_ge(rinv_ready, b * NS + s + 1)
                for k in range(g):
                    part = prob[:, s % 4, k * n:(k + 1) * n]
                    last = nc.vector.tensor_scalar(part, part, rinv[:, s % 2, k:k + 1], None, ALU.mult)
                last.then_inc(pn_ready, 1)

            def gather(b, t_, i, steps):
                chunk = b * 8 + t_ * CH + i
                dve.wait_ge(pv_done, b * NS + steps)
                nc.vector.tensor_scalar(yT[:], YB[i % 2][:, 0:P], own[:, 0:1], None, ALU.mult).then_inc(yt_step, 1)
                for th in range(1, TH):
                    dve.wait_ge(yt_step, chunk * TH + th)
                    nc.vector.scalar_tensor_tensor(yT[:], YB[i % 2][:, th * P:(th + 1) * P], own[:, th:th + 1], yT[:],
                                                   ALU.mult, ALU.add).then_inc(yt_step, 1)

            def add(b, t_, i):
                dve.wait_ge(out_ready, b * 8 + t_ * CH + i + 1)
                part = x[:, bass.ds(b * (CH * C) + i * C, C)]
                nc.vector.tensor_tensor(part, part, FB[:, 0:C], ALU.add).then_inc(fb_read, 1)

            dve.wait_ge(loaded, ALL_LOADED)
            for n in range(5):
                take(0, 0, n)
            dve.wait_ge(bo_added, 1)

            def body(b, final):
                for s in range(NS + L2 + 1):
                    if s < NS:
                        hs, n, i = heads(s)
                        g = len(hs)
                        dve.wait_ge(s_ready, b * NS + s + 1)
                        nc.vector.tensor_reduce(mx[:, s % 4, 0:g], SC[s % 3][:, 0:g * n].rearrange("p (g n) -> p g n", g=g),
                                                AX.X, ALU.max).then_inc(mx_step, 1)
                        dve.wait_ge(mx_step, (b * NS + s) * 2 + 1)
                        nc.vector.tensor_scalar(nmx[:, s % 4, 0:g], mx[:, s % 4, 0:g], -SCALE, None, ALU.mult).then_inc(mx_step, 1)
                    if 1 <= s < NS + 1:
                        normalise(b, s - 1)
                    k = s - L2
                    if k == NS or (k > 0 and place(k)[2] == 0):
                        t_, i = place(k - 1)[:2]
                        gather(b, t_, i, k)
                    if 0 < k <= NS:
                        t_, i, n, m = place(k - 1)
                        if n == 2 and (t_, i) != (0, 0):
                            add(b, *((t_, i - 1) if i else (t_ - 1, CH - 1)))
                        p = prefetch(k - 1)
                        if p is not None and not (final and t_ == 1):
                            take(b * 2 + t_ + 1, 1 - t_, p)
                add(b, 1, CH - 1)
            iterations(dve, body)


def dequantise(nc, ctx, sem, keep, ins):
    def sb(n, shape, dt=FP32):
        return ctx.enter_context(nc.sbuf_tensor("dq_" + n, shape, dt))
    qg, qu, qd = sb("qg", [P, CK, FF2 * P], INT32), sb("qu", [P, CK, FF2 * P], INT32), sb("qd", [P, FF2, C], INT32)
    sd = sb("sd", [P, C])
    loaded, step = sem("dq_loaded"), sem("dq_step")

    def sync(sp):
        for dst, src in ((qg[:], ins["q_gate"]), (qu[:], ins["q_up"]), (sd[:], ins["s_down"].partition_broadcast(P)),
                         (qd[:], ins["q_down"]), (keep["s_gate"][:], ins["s_gate"]), (keep["s_up"][:], ins["s_up"])):
            sp.dma_start(dst, src).then_inc(loaded, 16)

    def gpsimd(pool):
        pool.wait_ge(loaded, 16 * 6)
        nc.gpsimd.tensor_scalar(keep["wg2"][:], qg[:], -ZERO_POINT, None, ALU.add)
        nc.gpsimd.tensor_scalar(keep["wu2"][:], qu[:], -ZERO_POINT, None, ALU.add)
        nc.gpsimd.tensor_scalar(keep["wd2"][:], qd[:], -ZERO_POINT, None, ALU.add).then_inc(step, 1)
        pool.wait_ge(step, 1)
        nc.gpsimd.tensor_tensor(keep["wd2"][:], keep["wd2"][:], sd[:].unsqueeze(1).broadcast_to((P, FF2, C)), ALU.mult)
    return sync, gpsimd


class Semaphores:
    def __init__(self, nc, ctx):
        self.nc, self.ctx, self.found = nc, ctx, {}

    def __call__(self, name):
        if name not in self.found:
            self.found[name] = self.ctx.enter_context(self.nc.semaphore(name))
        return self.found[name]


def program(nc, ins, out):
    with ExitStack() as ctx:
        sem = Semaphores(nc, ctx)
        banks = [ctx.enter_context(nc.psum_tensor(f"bank{i}", [P, 512], FP32)) for i in range(8)]

        def sb(stack, n, shape, dt=FP32):
            return stack.enter_context(nc.sbuf_tensor(n, shape, dt))
        keep = {"x": sb(ctx, "x", [P, TILES * C]), "xnT": sb(ctx, "xnT", [P, CK, B * T]), "ident": sb(ctx, "ident", [P, P]),
                "ones1": sb(ctx, "ones1", [P, 1]), "eye_b": sb(ctx, "eye_b", [P, P], BF16), "cmask": sb(ctx, "cmask", [P, P], BF16)}
        with ExitStack() as first:
            keep["gates"] = sb(first, "gates", [P, (ITERS + 1) * NG * U])
            keep["wout"] = sb(first, "wout", [P, (NK + 1) * HH * C])
            keep["convw"] = sb(first, "convw", [P, (NK + 1) * NCV * TAPS])
            keep["tri"] = sb(first, "tri", [P, 4, P])
            keep["negmask"] = sb(first, "negmask", [P, GU * P], BF16)
            keep["first"] = sb(first, "first", [P, HALF])
            keep["odd"] = sb(first, "odd", [P, 1])
            keep["lmask"] = sb(first, "lmask", [P, len(LEVELS), HALF])
            first_norm_and_gates(nc, sem, banks, keep, ins)
            delta_rule(nc, sem, banks, keep, ins)
        with ExitStack() as second:
            for name in ("wg1", "wu1"):
                keep[name] = sb(second, name, [P, CK, SPL_OUT])
            keep["wd1"] = sb(second, "wd1", [P, FF1, C])
            spline_weights(nc, sem, banks, keep, ins)
            norm_phase(nc, sem, banks, keep, "ln2")
            ffn(nc, sem, banks, keep, "ff1", keep["wg1"], keep["wu1"], keep["wd1"], SPL_OUT)
        norm_phase(nc, sem, banks, keep, "ln3")
        with ExitStack() as third:
            for name in ("wg2", "wu2"):
                keep[name] = sb(third, name, [P, CK, FF2 * P])
            keep["wd2"] = sb(third, "wd2", [P, FF2, C])
            keep["s_gate"], keep["s_up"] = sb(third, "s_gate", [P, FF2]), sb(third, "s_up", [P, FF2])
            attention(nc, sem, banks, keep, ins)
            norm_phase(nc, sem, banks, keep, "ln4")
            ffn(nc, sem, banks, keep, "ff2", keep["wg2"], keep["wu2"], keep["wd2"], FF2 * P, keep["s_gate"], keep["s_up"])
        x = keep["x"]
        written = sem("written")
        block = ctx.enter_context(nc.Block())

        @block.sync
        def _(sp):
            for b in range(B):
                sp.dma_start(out[b * T:(b + 1) * T, :].rearrange("(j p) c -> p j c", p=P),
                             x[:, CH * b * C:CH * (b + 1) * C].rearrange("p (j c) -> p j c", c=C)).then_inc(written, 16)
            sp.wait_ge(written, 16 * B)


def layouts(d):
    f = lambda a: np.ascontiguousarray(a)
    r = np.arange(P)
    h = {}
    h["x"] = f(d["L0_attn_x"]).reshape(B * T, C)

    def by_channel(w):
        return w.T.reshape(CK, P, -1).transpose(1, 0, 2)
    wqkv, wz = d["L0_attn_W_qkv"], d["L0_attn_W_z"]
    heads = []
    conv = []
    for k in range(NK):
        q, kk = slice(k * D, (k + 1) * D), slice(NK * D + k * D, NK * D + (k + 1) * D)
        v = slice(2 * NK * D + HH * k * D, 2 * NK * D + HH * (k + 1) * D)
        z = slice(HH * k * D, HH * (k + 1) * D)
        heads.append(by_channel(np.concatenate([wqkv[kk], wqkv[q], wqkv[v], wz[z]])))
        cw = d["L0_attn_conv_w"]
        conv.append(np.concatenate([cw[kk], cw[q], cw[v]]).reshape(NCV, P, TAPS).transpose(1, 0, 2))
    h["w_heads"] = f(np.stack(heads))
    h["conv_w"] = f(np.stack(conv, 1)).reshape(P, NK * NCV * TAPS)
    h["w_ab"] = f(by_channel(np.concatenate([d["L0_attn_W_b"], d["L0_attn_W_a"]])))
    h["dt_bias"], h["A_log"] = f(d["L0_attn_dt_bias"]), f(d["L0_attn_A_log"])
    h["norm_w"] = f(d["L0_attn_norm_w"]).reshape(P, 1)
    h["w_out"] = f(d["L0_attn_W_out"].T.reshape(NV, D, C).transpose(1, 0, 2)).reshape(P, NV * C)
    j, t = r[:, None], r[None, :]
    h["ident"] = np.eye(P, dtype=np.float32)
    h["tri"] = f(np.stack([j <= t, j < t, j > t, j >= 0 * t], 1).astype(np.float32))
    col = np.arange(HALF)
    h["first"] = f(-(j // 2 == col[None, :]).astype(np.float32))
    h["odd"] = f((j % 2).astype(np.float32))
    h["lmask"] = f(np.stack([(j // b == 2 * (col // b)[None, :] + 1) for b in LEVELS], 1).astype(np.float32))
    points, basis = spline_constants()
    cps = np.stack([d[f"L0_ffn_{n}_cp"][points] for n in ("gate", "up", "down")])
    h["spl_points"] = f(cps.reshape(3, SPL_TAPS, SPL_TILES, P).transpose(3, 2, 0, 1))
    h["spl_basis"] = f(basis.reshape(SPL_TAPS, SPL_TILES, P, P).transpose(1, 2, 0, 3))
    row = np.arange(2 * P)
    kv = row // (GRP * HD) * HD + row % HD
    turn = lambda c: c // HD * HD + (c % HD + HD // 2) % HD
    q, k = d["L1_attn_Wq"], d["L1_attn_Wk"]
    four = [q, q[turn(row)], k[kv], k[turn(kv)]]
    h["at_w"] = f(np.stack([np.stack([by_channel(a[t_ * P:(t_ + 1) * P]) for a in four], 1) for t_ in range(2)]))
    bq, bk = d["L1_attn_bq"], d["L1_attn_bk"]
    h["at_bias"] = f(np.stack([bq, bq[turn(row)], bk[kv], bk[turn(kv)]], -1).reshape(2, P, 4).transpose(1, 0, 2))
    h["at_wv"] = f(by_channel(d["L1_attn_Wv"]))
    h["at_bv"], h["at_bo"] = f(d["L1_attn_bv"]), f(d["L1_attn_bo"])
    h["at_wo"] = f(d["L1_attn_Wo"].T.reshape(2, TH, GRP, HD, C).transpose(2, 1, 3, 0, 4)).reshape(P, 2 * C)
    h["own"] = f((r[:, None] // HD % TH == np.arange(TH)).astype(np.float32))
    jj = (r % HD % (HD // 2)).astype(np.float32)
    theta = np.float32(ROPE_BASE) ** (np.float32(-2.0) * jj / np.float32(HD))
    ang = (np.arange(T, dtype=np.float32) + 1.0)[None, :] * theta.astype(np.float32)[:, None]
    h["cosines"] = f(np.cos(ang.astype(np.float64)).astype(np.float32))
    sign = np.where(r % HD < HD // 2, -1.0, 1.0)[:, None]
    h["sines"] = f((sign * np.sin(ang.astype(np.float64))).astype(np.float32))
    h["gmask"] = f(((r % (GRP * HD)) // HD == np.arange(GRP)[:, None]).T.astype(np.float32))

    def padded(a):
        return np.concatenate([a, np.zeros((FF2 * P - DIM2, *a.shape[1:]), a.dtype)])
    h["q_gate"], h["q_up"] = f(by_channel(padded(d["L1_ffn_wq_gate"]))), f(by_channel(padded(d["L1_ffn_wq_up"])))

    def inner_tiles(a):
        return f(np.moveaxis(padded(a).reshape(FF2, P, *a.shape[1:]), 0, 1))
    h["q_down"] = inner_tiles(d["L1_ffn_wq_down"].T)
    h["s_gate"], h["s_up"], h["s_down"] = inner_tiles(d["L1_ffn_s_gate"]), inner_tiles(d["L1_ffn_s_up"]), f(d["L1_ffn_s_down"])
    return h


def kernel(**inputs):
    import concourse.bacc as bacc
    from concourse.bass_utils import run_bass_kernel_spmd
    nc = bacc.Bacc("TRN2", target_bir_lowering=False, num_devices=1)
    arrays, ins = {}, {}
    for name, a in layouts({k: np.asarray(v) for k, v in inputs.items()}).items():
        arrays[f"in_{name}"] = a
        ins[name] = nc.dram_tensor(f"in_{name}", a.shape, mybir.dt.from_np(a.dtype), kind="ExternalInput").ap()
    out = nc.dram_tensor("out_y", (B * T, C), FP32, kind="ExternalOutput").ap()
    program(nc, ins, out)
    r = run_bass_kernel_spmd(nc, [arrays], core_ids=[0])
    return r.results[0]["out_y"].reshape(B, T, C)
```
